# Optimizing a Trainium2 kernel written in Bass

```python
import numpy as np
import jax
import jax.numpy as jnp

def _softmax(x, axis=-1):
    return jax.nn.softmax(x, axis=axis)

def _gelu(x):
    return jax.nn.gelu(x, approximate=True)

def _silu(x):
    return jax.nn.silu(x)

def _sigmoid(x):
    return jax.nn.sigmoid(x)

def _layernorm(x, axis=-1, eps=1e-05):
    m = jnp.mean(x, axis=axis, keepdims=True)
    v = jnp.var(x, axis=axis, keepdims=True)
    return (x - m) / jnp.sqrt(v + eps)

def _scatter_add(tgt, idx, src, axis=0):
    return tgt.at[idx].add(src)

def _segment_sum(src, seg, n):
    return jax.ops.segment_sum(src, seg, n)
kernel_name = 'mk_perceiver_d1_seqx_r2_09b28c'

def setup_inputs(seed: int=0):
    np.random.seed(seed)
    _w = jnp.asarray

    def _rec_inputs():
        import jax
        import jax.numpy as jnp
        _rk = jax.random.key(seed)
        x = -0.0002928 + 1 * jax.random.normal(jax.random.fold_in(_rk, 1), (8, 128, 512), jnp.float32)
        _lenS = 128 - jax.random.randint(jax.random.fold_in(_rk, 7), (8,), 0, max(1, 128 // 4) + 1, jnp.int32)
        _lenS2 = 2048 - jax.random.randint(jax.random.fold_in(_rk, 8), (8,), 0, max(1, 2048 // 4) + 1, jnp.int32)
        _ctx_1024P = jax.random.normal(jax.random.fold_in(_rk, 11), (8, 16, 512), jnp.float32)
        _ctx_1024c = jax.random.dirichlet(jax.random.fold_in(_rk, 511), 0.3 * jnp.ones((16,), jnp.float32), (8, 2048))
        _ctx_1024t = jnp.einsum('bsk,bkd->bsd', _ctx_1024c, _ctx_1024P)
        _ctx_1024t = _ctx_1024t * jax.lax.rsqrt(jnp.mean(jnp.square(_ctx_1024t)) + 1e-12) * 0.953939
        ctx_1024 = -1.52775e-05 + 0.999936 * (_ctx_1024t + 0.3 * jax.random.normal(jax.random.fold_in(_rk, 611), (8, 2048, 512), jnp.float32))
        return (x, ctx_1024)
    x, ctx_1024 = _rec_inputs()

    def _L0_xattn_setup():
        import jax, jax.numpy as jnp
        import numpy as np
        DIM = 512
        NUM_HEADS = 8
        HEAD_DIM = 64
        INNER = NUM_HEADS * HEAD_DIM
        key = jax.random.key(seed)
        ks = jax.random.split(key, 7)
        B, N, M = (8, 256, 2048)
        x = jax.random.normal(ks[0], (B, N, DIM), dtype=jnp.float32)
        context = jax.random.normal(ks[1], (B, M, DIM), dtype=jnp.float32)
        s_in = 1.0 / np.sqrt(DIM)
        s_inner = 1.0 / np.sqrt(INNER)
        Wq = jax.random.normal(ks[2], (DIM, INNER), dtype=jnp.float32) * s_in
        Wk = jax.random.normal(ks[3], (DIM, INNER), dtype=jnp.float32) * s_in
        Wv = jax.random.normal(ks[4], (DIM, INNER), dtype=jnp.float32) * s_in
        Wo = jax.random.normal(ks[5], (INNER, DIM), dtype=jnp.float32) * s_inner
        bo = jax.random.normal(ks[6], (DIM,), dtype=jnp.float32) * 0.01
        return {'x': x, 'context': context, 'Wq': Wq, 'Wk': Wk, 'Wv': Wv, 'Wo': Wo, 'bo': bo}
    _L0_xattn_all = _L0_xattn_setup()
    _L0_xattn_in = {k: v for k, v in _L0_xattn_all.items() if k in ('Wq', 'Wk', 'Wv', 'Wo', 'bo')}
    del _L0_xattn_all

    def _L0_attn_setup():
        import jax, jax.numpy as jnp
        import numpy as np
        D_MODEL, N_HEADS, N_KV, HEAD_DIM, D_LAT = (512, 8, 2, 128, 32)
        N_REP = N_HEADS // N_KV
        B, T = (2, 1024)
        key = jax.random.key(seed)
        ks = jax.random.split(key, 8)
        s = lambda fan_in: 1.0 / np.sqrt(fan_in)
        return {'x': jax.random.normal(ks[0], (B, T, D_MODEL), jnp.float32), 'wq': jax.random.normal(ks[1], (D_MODEL, N_HEADS * HEAD_DIM), jnp.float32) * s(D_MODEL), 'wk_down': jax.random.normal(ks[2], (D_MODEL, N_KV * D_LAT), jnp.float32) * s(D_MODEL), 'wv_down': jax.random.normal(ks[3], (D_MODEL, N_KV * D_LAT), jnp.float32) * s(D_MODEL), 'wk_up': jax.random.normal(ks[4], (D_LAT, HEAD_DIM), jnp.float32) * s(D_LAT), 'wv_up': jax.random.normal(ks[5], (D_LAT, HEAD_DIM), jnp.float32) * s(D_LAT), 'wo': jax.random.normal(ks[6], (N_HEADS * HEAD_DIM, D_MODEL), jnp.float32) * s(N_HEADS * HEAD_DIM)}
    _L0_attn_all = _L0_attn_setup()
    _L0_attn_in = {k: v for k, v in _L0_attn_all.items() if k in ('wq', 'wk_down', 'wv_down', 'wk_up', 'wv_up', 'wo')}
    del _L0_attn_all

    def _L0_ffn_setup():
        import jax, jax.numpy as jnp
        import numpy as np
        TOP_K = 2

        def _gelu(x):
            return jax.nn.gelu(x, approximate=False)
        key = jax.random.key(seed)
        ks = jax.random.split(key, 6)
        B, S, D, F, E = (2, 1024, 512, 1024, 8)
        sc_g = 1.0 / np.sqrt(D)

        def xav(k, shape, fan_in, fan_out):
            lim = np.sqrt(6.0 / (fan_in + fan_out))
            return jax.random.uniform(k, shape, jnp.float32, -lim, lim)
        return {'x': jax.random.normal(ks[0], (B, S, D), jnp.float32), 'Wg': xav(ks[1], (D, E), D, E), 'Wu': xav(ks[2], (E, D, F), D, F), 'Wd': xav(ks[3], (E, F, D), F, D), 'W1': xav(ks[4], (D, F), D, F), 'W2': xav(ks[5], (F, D), F, D)}
    _L0_ffn_all = _L0_ffn_setup()
    _L0_ffn_in = {k: v for k, v in _L0_ffn_all.items() if k in ('Wg', 'Wu', 'Wd', 'W1', 'W2')}
    del _L0_ffn_all
    return {'x': x, 'ctx_1024': ctx_1024, 'L0_xattn_Wq': _L0_xattn_in['Wq'], 'L0_xattn_Wk': _L0_xattn_in['Wk'], 'L0_xattn_Wv': _L0_xattn_in['Wv'], 'L0_xattn_Wo': _L0_xattn_in['Wo'], 'L0_xattn_bo': _L0_xattn_in['bo'], 'L0_attn_wq': _L0_attn_in['wq'], 'L0_attn_wk_down': _L0_attn_in['wk_down'], 'L0_attn_wv_down': _L0_attn_in['wv_down'], 'L0_attn_wk_up': _L0_attn_in['wk_up'], 'L0_attn_wv_up': _L0_attn_in['wv_up'], 'L0_attn_wo': _L0_attn_in['wo'], 'L0_ffn_Wg': _L0_ffn_in['Wg'], 'L0_ffn_Wu': _L0_ffn_in['Wu'], 'L0_ffn_Wd': _L0_ffn_in['Wd'], 'L0_ffn_W1': _L0_ffn_in['W1'], 'L0_ffn_W2': _L0_ffn_in['W2']}

def reference(x, ctx_1024, L0_xattn_Wq, L0_xattn_Wk, L0_xattn_Wv, L0_xattn_Wo, L0_xattn_bo, L0_attn_wq, L0_attn_wk_down, L0_attn_wv_down, L0_attn_wk_up, L0_attn_wv_up, L0_attn_wo, L0_ffn_Wg, L0_ffn_Wu, L0_ffn_Wd, L0_ffn_W1, L0_ffn_W2):
    import jax
    import jax.numpy as jnp

    def _L0_xattn_ref(x, context, Wq, Wk, Wv, Wo, bo):
        import jax, jax.numpy as jnp
        import numpy as np
        DIM = 512
        NUM_HEADS = 8
        HEAD_DIM = 64
        INNER = NUM_HEADS * HEAD_DIM
        B, N, _ = x.shape
        M = context.shape[1]
        scale = HEAD_DIM ** (-0.5)
        q = (x @ Wq).reshape(B, N, NUM_HEADS, HEAD_DIM).transpose(0, 2, 1, 3)
        k = (context @ Wk).reshape(B, M, NUM_HEADS, HEAD_DIM).transpose(0, 2, 1, 3)
        v = (context @ Wv).reshape(B, M, NUM_HEADS, HEAD_DIM).transpose(0, 2, 1, 3)
        attn = jax.nn.softmax(jnp.einsum('bhnd,bhmd->bhnm', q, k) * scale, axis=-1)
        out = jnp.einsum('bhnm,bhmd->bhnd', attn, v)
        out = out.transpose(0, 2, 1, 3).reshape(B, N, INNER)
        return out @ Wo + bo

    def _L0_attn_ref(x, wq, wk_down, wv_down, wk_up, wv_up, wo):
        import jax, jax.numpy as jnp
        import numpy as np
        D_MODEL, N_HEADS, N_KV, HEAD_DIM, D_LAT = (512, 8, 2, 128, 32)
        N_REP = N_HEADS // N_KV
        B, T = (2, 1024)
        Bq, Tq, _ = x.shape
        scale = HEAD_DIM ** (-0.5)
        q = (x @ wq).reshape(Bq, Tq, N_KV, N_REP, HEAD_DIM)
        k_lat = (x @ wk_down).reshape(Bq, Tq, N_KV, D_LAT)
        v_lat = (x @ wv_down).reshape(Bq, Tq, N_KV, D_LAT)
        k = jnp.einsum('bkhl,ld->bkhd', k_lat, wk_up)
        v = jnp.einsum('bkhl,ld->bkhd', v_lat, wv_up)
        scores = jnp.einsum('bqhrd,bkhd->bhrqk', q, k) * scale
        causal = jnp.tril(jnp.ones((Tq, Tq), dtype=bool))
        scores = jnp.where(causal, scores, jnp.finfo(scores.dtype).min)
        probs = jax.nn.softmax(scores, axis=-1)
        y = jnp.einsum('bhrqk,bkhd->bqhrd', probs, v)
        y = y.reshape(Bq, Tq, N_HEADS * HEAD_DIM)
        return y @ wo

    def _L0_ffn_ref(x, Wg, Wu, Wd, W1, W2):
        import jax, jax.numpy as jnp
        import numpy as np
        TOP_K = 2

        def _gelu(x):
            return jax.nn.gelu(x, approximate=False)
        B, S, D = x.shape
        E = Wu.shape[0]
        T = B * S
        xt = x.reshape(T, D)
        probs = jax.nn.softmax(xt @ Wg, axis=-1)
        topv, topi = jax.lax.top_k(probs, TOP_K)
        topv = topv / jnp.sum(topv, axis=-1, keepdims=True)
        cw = jnp.zeros((T, E), x.dtype).at[jnp.arange(T)[:, None], topi].set(topv)
        h = _gelu(jnp.einsum('td,edf->tef', xt, Wu))
        y = jnp.einsum('tef,efd->ted', h, Wd)
        moe = jnp.einsum('ted,te->td', y, cw)
        shared = _gelu(xt @ W1) @ W2
        return (shared + moe).reshape(B, S, D)
    x = x + _L0_xattn_ref(_layernorm(x, axis=-1), ctx_1024, L0_xattn_Wq, L0_xattn_Wk, L0_xattn_Wv, L0_xattn_Wo, L0_xattn_bo)
    x = x + _L0_attn_ref(_layernorm(x, axis=-1), L0_attn_wq, L0_attn_wk_down, L0_attn_wv_down, L0_attn_wk_up, L0_attn_wv_up, L0_attn_wo)
    x = x + _L0_ffn_ref(_layernorm(x, axis=-1), L0_ffn_Wg, L0_ffn_Wu, L0_ffn_Wd, L0_ffn_W1, L0_ffn_W2)
    return x

_drawn_inputs = setup_inputs


def setup_inputs(seed=0):
    import zlib

    import numpy as np

    out = dict(_drawn_inputs(seed))
    spreads = {}
    factors = {'L0_xattn_bo': 2.975}
    for name, (base, spread) in spreads.items():
        noise = np.random.default_rng([zlib.crc32(name.encode()), seed]).standard_normal(out[name].shape)
        drawn = base * np.exp(spread * noise) if base else spread * noise
        out[name] = jnp.asarray(drawn.astype(out[name].dtype))
    for name, factor in factors.items():
        out[name] = (out[name] * factor).astype(out[name].dtype)
    return out
```

```python
from contextlib import ExitStack

import concourse.bass as bass
from concourse import mybir

F32 = mybir.dt.float32
F32R = mybir.dt.float32r
U32 = mybir.dt.uint32
ALU = mybir.AluOpType
ACT = mybir.ActivationFunctionType
AX_X = mybir.AxisListType.X

P = 128
EPS = 1e-5

B, T, D = 8, 128, 512
M = 2048
XH, XD = 8, 64
SH, SKV, SD, LAT = 8, 2, 128, 32
REP = SH // SKV
E, F = 8, 1024
DC = D // P
PAIRS = XH // 2
QT = 512
NQ = M // QT
MT = M // P
X_SCALE = XD ** -0.5
S_SCALE = SD ** -0.5

AHEAD = 1


def cross_attention(nc, x_ap, ctx_ap, wq_ap, wk_ap, wv_ap, q_dram, o_dram):
    with ExitStack() as ctx:
        def sb(name, shape, dt):
            return ctx.enter_context(nc.sbuf_tensor(name, shape, dt))

        def sem(name):
            return ctx.enter_context(nc.semaphore(name))

        wk = sb("wk", [P, 2, DC, D], F32R)
        wv = sb("wv", [P, 2, DC, D], F32R)
        stage = sb("stage", [P, 2, 2, QT], F32)
        ctx_h = sb("ctx_h", [P, 2, DC, QT], F32R)
        ctx_l = sb("ctx_l", [P, 2, DC, QT], F32R)
        kT = sb("kT", [P, 2, PAIRS, M], F32R)
        vt = sb("vt", [P, MT, D], F32)
        qa = sb("qa", [P, XH, T], F32R)
        qb = sb("qb", [P, XH, T], F32R)
        probs = sb("probs", [P, 2, M], F32)
        pT = sb("pT", [P, 2, MT, P], F32)
        on = sb("on", [P, PAIRS, P], F32)
        ident = sb("ident", [P, P], F32)
        one = sb("one", [P, 1], F32)
        mhalf = sb("mhalf", [P, 1], F32)
        spread = sb("spread", [P, XH, XD], F32)
        smax = sb("smax", [P, XH, 2], F32)
        nmax = sb("nmax", [P, XH], F32)
        rsum = sb("rsum", [P, XH, 2], F32)
        rtot = sb("rtot", [P, XH], F32)
        rinv = sb("rinv", [P, XH], F32)
        stats = sb("stats", [P, B, 6], F32)
        mv = sb("mv", [P, B, 2], F32)
        rstd = sb("rstd", [P, B], F32)

        x_all = probs[:, :, :].rearrange("p a (b d) -> p (a b) d", d=D)
        pT_flat = pT[:, :, :, :].rearrange("p a t m -> p a (t m)")
        wq = pT_flat[:, 0, :].rearrange("p (c n) -> p c n", c=DC)
        xnT = pT_flat[:, 1, :].rearrange("p (c n) -> p c n", c=DC)
        qa_flat = qa[:, :, :].rearrange("p (s h) t -> p s (h t)", s=2)
        qb_flat = qb[:, :, :].rearrange("p (s h) t -> p s (h t)", s=2)

        ps_s = ctx.enter_context(nc.psum_tensor("ps_s", [P, 4, 512], F32))
        ps_t = ctx.enter_context(nc.psum_tensor("ps_t", [P, 2, 4, P], F32))
        ps_o = ctx.enter_context(nc.psum_tensor("ps_o", [P, PAIRS, P], F32))
        ps_r = ctx.enter_context(nc.psum_tensor("ps_r", [P, PAIRS, P], F32))

        x_in = sem("x_in")
        wq_in = sem("wq_in")
        ident_ok = sem("ident_ok")
        bn_done = sem("bn_done")
        rstd_done = sem("rstd_done")
        xn_done = sem("xn_done")
        xT_done = sem("xT_done")
        xT_copied = sem("xT_copied")
        qp_done = sem("qp_done")
        q_hi = sem("q_hi")
        q_lo = sem("q_lo")
        q_stored = [sem("q_stored0"), sem("q_stored1")]
        raw_in = [sem("raw_in0"), sem("raw_in1")]
        hi_done = sem("hi_done")
        split_done = sem("split_done")
        proj_done = sem("proj_done")
        k_hi = sem("k_hi")
        k_lo = sem("k_lo")
        v_copied = sem("v_copied")
        q_in = sem("q_in")
        s_done = sem("s_done")
        max_done = sem("max_done")
        nmax_done = sem("nmax_done")
        exp_done = sem("exp_done")
        t_done = sem("t_done")
        pT_even = sem("pT_even")
        pT_odd = sem("pT_odd")
        pv_done = sem("pv_done")
        sum_done = sem("sum_done")
        spread_done = sem("spread_done")
        r_done = sem("r_done")
        r_copied = sem("r_copied")
        on_done = sem("on_done")
        o_stored = sem("o_stored")

        HB = B // 2
        HT = HB * T
        NW = 2 * DC // 2
        LB = NQ * DC // 2
        GQ = PAIRS + QT // P
        GB = NQ * GQ

        block = ctx.enter_context(nc.Block())

        @block.sync
        def _(sp):
            sp.dma_start(x_all, x_ap.rearrange("b t d -> t b d")).then_inc(x_in, 16)
            sp.dma_start(wq, wq_ap.rearrange("(c p) n -> p c n", p=P)).then_inc(wq_in, 16)
            for n in range(NW):
                w_ap, c = (wk_ap, wv_ap)[n // 2], 2 * (n % 2)
                if n >= 2:
                    sp.wait_ge(split_done, n - 1)
                sp.dma_start(stage[:, n % 2], w_ap[c * P:(c + 2) * P, :].rearrange("(c p) n -> p c n", p=P)) \
                    .then_inc(raw_in[n % 2], 16)
            with sp.Fori(0, B) as b:
                for k in range(LB):
                    sp.wait_ge(split_done, b * LB + (NW + k - 1))
                    sp.dma_start(stage[:, k % 2],
                                 ctx_ap[bass.ds(b, 1), k // 2, :, 2 * (k % 2):2 * (k % 2) + 2, :]
                                 .rearrange("o p c m -> (o p) c m")).then_inc(raw_in[k % 2], 16)

        @block.gpsimd
        def _(pool):
            for count in (s_done, exp_done, pT_even, pT_odd, on_done, o_stored):
                pool.sem_inc(count, AHEAD)
            pool.memset(one[:, :], 1.0).then_inc(ident_ok, 1)
            pool.memset(mhalf[:, :], -0.5).then_inc(ident_ok, 1)
            pool.memset(ident[:, :], 0.0).then_inc(ident_ok, 1)
            pool.wait_ge(ident_ok, 3)
            pool.affine_select(out=ident[:, :], in_=ident[:, :], compare_op=ALU.not_equal, fill=1.0, base=0,
                               pattern=[[-1, P]], channel_multiplier=1).then_inc(ident_ok, 1)
            pool.wait_ge(ident_ok, 4)

            def split(hi, lo, slot, loads, before):
                pool.wait_ge(raw_in[slot], loads)
                nc.gpsimd.tensor_tensor(hi, stage[:, slot], one[:, 0:1].unsqueeze(2).broadcast_to([P, 2, QT]),
                                        ALU.mult).then_inc(hi_done, 1)
                pool.wait_ge(hi_done, before + 1)
                nc.gpsimd.tensor_tensor(lo, stage[:, slot], hi, ALU.subtract).then_inc(split_done, 1)

            for n in range(NW):
                w, c = (wk, wv)[n // 2], 2 * (n % 2)
                split(w[:, 0, c:c + 2, :], w[:, 1, c:c + 2, :], n % 2, 16 * (n // 2 + 1), n)
                if n == 0:
                    pool.wait_ge(bn_done, 2 * B + 1)
                    nc.gpsimd.tensor_tensor(rstd[:, :], rstd[:, :], mhalf[:, :].broadcast_to([P, B]), ALU.pow) \
                        .then_inc(rstd_done, 1)
            with pool.Fori(0, B) as b:
                for k in range(LB):
                    g, c = k // 2, 2 * (k % 2)
                    if c == 0:
                        pool.wait_ge(proj_done, b * GB + GQ * (g + 1))
                    split(ctx_h[:, g % 2, c:c + 2, :], ctx_l[:, g % 2, c:c + 2, :], k % 2,
                          b * (16 * LB // 2) + 16 * (NW // 2 + k // 2 + 1), b * LB + (NW + k))

        @block.tensor
        def _(pe):
            pe.wait_ge(ident_ok, 4)
            for half in range(2):
                for i in range(HB):
                    n = half * HB + i
                    pe.wait_ge(xn_done, n + 1)
                    if n >= 2:
                        pe.wait_ge(xT_copied, n - 1)
                    for c in range(DC):
                        last = nc.tensor.transpose(ps_t[:, n % 2, c, :], x_all[:, n, c * P:(c + 1) * P], ident[:, :])
                    last.then_inc(xT_done, 1)
                pe.wait_ge(wq_in, 16)
                pe.wait_ge(xT_copied, (half + 1) * HB)
                for p in range(PAIRS):
                    if half:
                        pe.wait_ge(q_lo, p + 1)
                    for c in range(DC):
                        last = nc.tensor.matmul(ps_s[:, p, :], wq[:, c, p * P:(p + 1) * P], xnT[:, c, :],
                                                start=(c == 0), stop=(c == DC - 1))
                    last.then_inc(qp_done, 1)
            pe.wait_ge(q_lo, 2 * PAIRS)

            def three(out, w_hi, w_lo, m_hi, m_lo):
                for c in range(DC):
                    for k, (w, m) in enumerate(((w_hi, m_hi), (w_hi, m_lo), (w_lo, m_hi))):
                        mm = nc.tensor.matmul(out, w(c), m(c), start=(c + k == 0), stop=(c == DC - 1 and k == 2))
                return mm

            with pe.Fori(0, B) as b:
                pe.wait_ge(exp_done, AHEAD + b * (2 * XH))
                for g in range(NQ):
                    pe.wait_ge(split_done, b * LB + (NW + 2 * (g + 1)))
                    h, l = ctx_h[:, g % 2], ctx_l[:, g % 2]
                    for p in range(PAIRS):
                        if g:
                            pe.wait_ge(v_copied, b * MT + (4 * (g - 1) + p + 1))
                        cols = slice(p * P, (p + 1) * P)
                        three(ps_s[:, p, :], lambda c: wk[:, 0, c, cols], lambda c: wk[:, 1, c, cols],
                              lambda c: h[:, c, :], lambda c: l[:, c, :]).then_inc(proj_done, 1)
                    for t in range(4):
                        pe.wait_ge(k_lo, b * (NQ * PAIRS) + (PAIRS * g + t + 1))
                        rows = slice(t * P, (t + 1) * P)
                        mm = three(ps_s[:, t, :], lambda c: h[:, c, rows], lambda c: l[:, c, rows],
                                   lambda c: wv[:, 0, c, :], lambda c: wv[:, 1, c, :])
                        mm.then_inc(proj_done, 1)

                def scores(h):
                    for j in range(4):
                        if h:
                            pe.wait_ge(exp_done, AHEAD + b * (2 * XH) + (2 * (h - 1) + j // 2 + 1))
                        keys = kT[:, h % 2, h // 2, j * 512:(j + 1) * 512]
                        nc.tensor.matmul(ps_s[:, j, :], qa[:, h, :], keys, start=True, stop=False)
                        mm = nc.tensor.matmul(ps_s[:, j, :], qb[:, h, :], keys, start=False, stop=True)
                        if j % 2:
                            mm.then_inc(s_done, 1)

                def transposes(h):
                    p, e = h // 2, h % 2
                    for j in range(4):
                        if j % 2 == 0:
                            pe.wait_ge(exp_done, AHEAD + b * (2 * XH) + (2 * h + j // 2 + 1))
                        own, other = (pT_odd, pT_even) if e else (pT_even, pT_odd)
                        if j >= 2:
                            pe.wait_ge(own, AHEAD + b * MT + (4 * p + j - 1))
                        else:
                            pe.wait_ge(other, AHEAD + b * MT + (4 * p + j + 3 if e else max(4 * p + j - 1, 0)))
                        for i in range(4):
                            mm = nc.tensor.transpose(ps_t[:, j % 2, i, :],
                                                     probs[:, e, (4 * j + i) * P:(4 * j + i + 1) * P], ident[:, :])
                        mm.then_inc(t_done, 1)

                def values(p, part):
                    if p == 0 and part == 0:
                        pe.wait_ge(on_done, AHEAD + b)
                        pe.wait_ge(v_copied, (b + 1) * MT)
                    pe.wait_ge(pT_even, AHEAD + b * MT + (4 * p + 2 * (part + 1)))
                    pe.wait_ge(pT_odd, AHEAD + b * MT + (4 * p + 2 * (part + 1)))
                    for t in range(8 * part, 8 * part + 8):
                        for e in range(2):
                            h = 2 * p + e
                            mm = nc.tensor.matmul(ps_o[e * XD:(e + 1) * XD, p, :], vt[:, t, h * XD:(h + 1) * XD],
                                                  pT[:, e, t, :], start=(t == 0), stop=(t == MT - 1))
                    return mm

                pe.wait_ge(k_lo, (b + 1) * (NQ * PAIRS))
                pe.wait_ge(v_copied, (b + 1) * MT)
                pe.wait_ge(q_in, (b + 1) * (16 * 8))
                for p in range(PAIRS):
                    scores(2 * p)
                    if p:
                        transposes(2 * p - 1)
                        values(p - 1, 0)
                    scores(2 * p + 1)
                    if p:
                        values(p - 1, 1)
                    transposes(2 * p)
                transposes(XH - 1)
                values(PAIRS - 1, 0)
                values(PAIRS - 1, 1).then_inc(pv_done, 1)
                pe.wait_ge(spread_done, b + 1)
                for p in range(PAIRS):
                    mm = nc.tensor.matmul(ps_r[:, p, :], spread[:, 2 * p:2 * p + 2, :].rearrange("p h d -> p (h d)"),
                                          ident[:, :], start=True, stop=True)
                mm.then_inc(r_done, 1)

        @block.scalar
        def _(act):
            act.sem_inc(proj_done, 2 * GQ)
            for n in range(2 * PAIRS):
                act.wait_ge(qp_done, n + 1)
                if n >= 2:
                    act.wait_ge(q_stored[n % 2], 16 * 2 * (n // 2))
                nc.scalar.activation(qa_flat[:, n % 2, :], ps_s[:, n % PAIRS, :], ACT.Copy).then_inc(q_hi, 1)
                act.wait_ge(q_lo, n + 1)
                half, p = n // PAIRS, n % PAIRS
                for w, src in enumerate((qa_flat, qb_flat)):
                    act.dma_start(q_dram[w, p, :, half * HT:(half + 1) * HT], src[:, n % 2, :].bitcast(F32)) \
                        .then_inc(q_stored[n % 2], 16)
            for done in q_stored:
                act.wait_ge(done, 16 * 2 * PAIRS)
            with act.Fori(0, B) as b:
                act.wait_ge(s_done, AHEAD + b * (2 * XH))
                for w, dst in enumerate((qa, qb)):
                    d = dst[:, :, :].bitcast(F32).rearrange("p (h e) t -> p h e t", e=2)
                    for e in range(2):
                        for to in range(2):
                            act.dma_start(d[to * XD:(to + 1) * XD, :, e, :],
                                          q_dram[w, :, e * XD:(e + 1) * XD, bass.ds(b * T, T)]
                                          .rearrange("h p t -> p h t")).then_inc(q_in, 16)
                for g in range(NQ):
                    keys = slice(g * QT, (g + 1) * QT)
                    for p in range(PAIRS):
                        act.wait_ge(proj_done, b * GB + (GQ * (g + 2) + p + 1))
                        nc.scalar.activation(kT[0:XD, 0, p, keys], ps_s[0:XD, p, :], ACT.Copy)
                        nc.scalar.activation(kT[XD:P, 1, p, keys], ps_s[XD:P, p, :], ACT.Copy).then_inc(k_hi, 1)
                    for t in range(4):
                        act.wait_ge(proj_done, b * GB + (GQ * (g + 2) + PAIRS + t + 1))
                        nc.scalar.activation(vt[:, 4 * g + t, :], ps_s[:, t, :], ACT.Copy).then_inc(v_copied, 1)

                def copy_odd(p):
                    for j in range(4):
                        act.wait_ge(t_done, b * (4 * XH) + (4 * (2 * p + 1) + j + 1))
                        nc.scalar.activation(pT[:, 1, 4 * j:4 * j + 4, :], ps_t[:, j % 2, :, :], ACT.Copy) \
                            .then_inc(pT_odd, 1)

                def exps(h):
                    act.wait_ge(nmax_done, b * XH + (h + 1))
                    for j in range(2):
                        nc.scalar.activation(probs[:, h % 2, j * 1024:(j + 1) * 1024], ps_s[:, 2 * j:2 * j + 2, :],
                                             ACT.Exp, bias=nmax[:, h:h + 1], scale=X_SCALE,
                                             accum_out=rsum[:, h, j:j + 1]).then_inc(exp_done, 1)

                for p in range(PAIRS):
                    if p:
                        copy_odd(p - 1)
                    exps(2 * p)
                    exps(2 * p + 1)
                copy_odd(PAIRS - 1)
                act.wait_ge(on_done, AHEAD + b + 1)
                act.dma_start(o_dram[bass.ds(b, 1)].rearrange("o p h t -> (o p) h t"), on[:, :, :]) \
                    .then_inc(o_stored, 16)
            act.wait_ge(o_stored, AHEAD + 16 * B)

        @block.vector
        def _(dve):
            dve.wait_ge(x_in, 16)
            for n in range(B):
                nc.vector.bn_stats(stats[:, n, :], x_all[:, n, :]).then_inc(bn_done, 1)
            for n in range(B):
                dve.wait_ge(bn_done, n + 1)
                nc.vector.bn_aggr(mv[:, n, :], stats[:, n, :]).then_inc(bn_done, 1)
            dve.wait_ge(bn_done, 2 * B)
            nc.vector.tensor_scalar(rstd[:, :], mv[:, :, 1], EPS, None, ALU.add).then_inc(bn_done, 1)
            dve.wait_ge(rstd_done, 1)
            for n in range(B):
                nc.vector.tensor_scalar(x_all[:, n, :], x_all[:, n, :], mv[:, n, 0:1], rstd[:, n:n + 1],
                                        ALU.subtract, ALU.mult).then_inc(xn_done, 1)

            def q_low(n):
                dve.wait_ge(q_hi, n + 1)
                nc.vector.tensor_tensor(qb_flat[:, n % 2, :], ps_s[:, n % PAIRS, :], qa_flat[:, n % 2, :],
                                        ALU.subtract).then_inc(q_lo, 1)

            for half in range(2):
                for i in range(HB):
                    n = half * HB + i
                    dve.wait_ge(xT_done, n + 1)
                    if half and i == 0:
                        dve.wait_ge(qp_done, PAIRS)
                    nc.vector.tensor_copy(xnT[:, :, i * T:(i + 1) * T], ps_t[:, n % 2, :, :]).then_inc(xT_copied, 1)
                for p in range(PAIRS):
                    q_low(half * PAIRS + p)

            with dve.Fori(0, B) as b:
                for g in range(NQ):
                    keys = slice(g * QT, (g + 1) * QT)
                    for p in range(PAIRS):
                        dve.wait_ge(k_hi, b * (NQ * PAIRS) + (PAIRS * g + p + 1))
                        nc.vector.tensor_tensor(kT[XD:P, 0, p, keys], ps_s[0:XD, p, :], kT[0:XD, 0, p, keys],
                                                ALU.subtract)
                        nc.vector.tensor_tensor(kT[0:XD, 1, p, keys], ps_s[XD:P, p, :], kT[XD:P, 1, p, keys],
                                                ALU.subtract).then_inc(k_lo, 1)

                def maxes(h):
                    for j in range(2):
                        dve.wait_ge(s_done, AHEAD + b * (2 * XH) + (2 * h + j + 1))
                        nc.vector.tensor_reduce(smax[:, h, j:j + 1], ps_s[:, 2 * j:2 * j + 2, :]
                                                .rearrange("p a n -> p (a n)"), AX_X, ALU.max).then_inc(max_done, 1)
                    dve.wait_ge(max_done, b * (2 * XH) + 2 * (h + 1))
                    nc.vector.tensor_scalar(nmax[:, h:h + 1], smax[:, h, 0:1], smax[:, h, 1:2], -X_SCALE,
                                            ALU.max, ALU.mult).then_inc(nmax_done, 1)

                def copy_even(p):
                    for j in range(4):
                        dve.wait_ge(t_done, b * (4 * XH) + (4 * (2 * p) + j + 1))
                        nc.vector.tensor_copy(pT[:, 0, 4 * j:4 * j + 4, :], ps_t[:, j % 2, :, :]).then_inc(pT_even, 1)

                for p in range(PAIRS):
                    maxes(2 * p)
                    maxes(2 * p + 1)
                    copy_even(p)
                dve.wait_ge(exp_done, AHEAD + (b + 1) * (2 * XH))
                nc.vector.tensor_tensor(rtot[:, :], rsum[:, :, 0], rsum[:, :, 1], ALU.add).then_inc(sum_done, 1)
                dve.wait_ge(sum_done, 2 * b + 1)
                nc.vector.reciprocal(rinv[:, :], rtot[:, :]).then_inc(sum_done, 1)
                dve.wait_ge(sum_done, 2 * b + 2)
                nc.vector.tensor_copy(spread[:, :, :], rinv[:, :].unsqueeze(2).broadcast_to([P, XH, XD])) \
                    .then_inc(spread_done, 1)
                dve.wait_ge(o_stored, AHEAD + b * 16)
                dve.wait_ge(r_done, b + 1)
                nc.vector.tensor_copy(on[:, :, :], ps_r[:, :, :]).then_inc(r_copied, 1)
                dve.wait_ge(r_copied, b + 1)
                nc.vector.tensor_tensor(on[:, :, :], ps_o[:, :, :], on[:, :, :], ALU.mult).then_inc(on_done, 1)


def self_attention(nc, x_ap, bo_ap, wxo_ap, wq_ap, wkd_ap, wvd_ap, wku_ap, wvu_ap, wo_ap, wg_ap, o_dram,
                   x2, xT_h, xT_l, logits):
    with ExitStack() as ctx:
        def sb(name, shape, dt=F32):
            return ctx.enter_context(nc.sbuf_tensor(name, shape, dt))

        def sem(name):
            return ctx.enter_context(nc.semaphore(name))

        NI = B // 2
        T2 = 2 * T
        DC2 = SH * SD // P
        wxo = sb("wxo", [P, PAIRS, D])
        wq = sb("wq2", [P, DC, SH * SD])
        wdown = sb("wdown", [P, DC, 4 * LAT])
        wup = sb("wup", [P, 4, SD])
        wo = sb("wo2", [P, DC2, D])
        wg = sb("wg", [P, DC, E])
        bo = sb("bo", [P, D])
        ident = sb("ident2", [P, P])
        mask = sb("mask", [P, P])
        mhalf = sb("mhalf2", [P, 1])
        o_in = sb("o_in", [P, 2, PAIRS, P])
        x1 = sb("x1", [P, 2, D])
        xn = sb("xn", [P, 2, D])
        xnT = sb("xnT", [P, DC, 2, T])
        qT = sb("qT", [P, SH, 2, T])
        lat = sb("lat", [P, 2, T])
        kT = sb("kT2", [P, SKV, 2, T])
        v = sb("v2", [P, 2, SKV, SD])
        sm = sb("sm", [P, 2, SKV, REP, T])
        pT = sb("pT2", [P, 2, SKV, REP, T])
        yT = sb("yT", [P, 2, SH, T])
        x3T = sb("x3T", [P, 2, DC, T])
        stats = sb("stats2", [P, 2, 2, 6])
        mv = sb("mv2", [P, 2, 2, 2])
        rstd = sb("rstd2", [P, 2, 2, 1])
        mx = sb("mx2", [P, 2, SKV, REP])
        sums = sb("sums2", [P, 2, SKV, REP])
        inv = sb("inv2", [P, 2, SKV, REP])
        one = sb("one2", [P, 1])
        hold = sb("hold", [P, 2, 2, 1])

        banks = [ctx.enter_context(nc.psum_tensor(f"bank{i}", [P, 512], F32)) for i in range(8)]

        uses = [["out0", "lat", "pT00", "wo0"], ["out1", "kT", "pT01", "wo1"],
                ["xT0", "v", "pT10", "x3T0"], ["xT1", "pT11", "x3T1"],
                ["q0", "sc00", "y00", "lg0"], ["q1", "sc01", "y01", "lg1"],
                ["q2", "sc10", "y10"], ["q3", "sc11", "y11"]]
        place = {name: (i, n) for i, names in enumerate(uses) for n, name in enumerate(names)}
        filled = [sem(f"filled{i}") for i in range(8)]
        copied = [sem(f"copied{i}") for i in range(8)]

        def bank(name, shape=None):
            ap = banks[place[name][0]][:, :]
            return ap

        def await_filled(eng, it, name):
            i, n = place[name]
            eng.wait_ge(filled[i], it * len(uses[i]) + (n + 1))

        def await_copied(eng, it, name):
            i, n = place[name]
            eng.wait_ge(copied[i], AHEAD + it * len(uses[i]) + (n + 1))

        def await_empty(eng, it, name):
            i, n = place[name]
            eng.wait_ge(copied[i], AHEAD + it * len(uses[i]) + n)

        w_in = sem("w_in")
        wup_zero = sem("wup_zero")
        consts = sem("consts")
        o_got = sem("o_got")
        x_got = sem("x_got")
        xb_done = sem("xb_done")
        dve_step = sem("dve_step")
        var_done = sem("var_done")
        rstd_done = sem("rstd_done2")
        xn_done = sem("xn_done2")
        sub_done = sem("sub_done")
        exp_done = sem("exp_done2")
        p_done = sem("p_done")
        hi_done = sem("hi_done2")
        lo_done = sem("lo_done2")

        weights = [(wxo, wxo_ap, "(c p) n -> p c n"), (wq, wq_ap, "(c p) n -> p c n"),
                   (wo, wo_ap, "(c p) n -> p c n"), (wg, wg_ap, "(c p) n -> p c n")]
        W_IN = 16 * (len(weights) + 2 + 4 + 1)

        block = ctx.enter_context(nc.Block())

        @block.sync
        def _(sp):
            sp.dma_start(bo[:, :], bo_ap.rearrange("(a n) -> a n", a=1).broadcast_to([P, D])).then_inc(w_in, 16)
            for w, ap, how in weights:
                sp.dma_start(w[:, :, :], ap.rearrange(how, p=P)).then_inc(w_in, 16)
            for i, ap in enumerate((wkd_ap, wvd_ap)):
                sp.dma_start(wdown[:, :, 2 * LAT * i:2 * LAT * (i + 1)], ap.rearrange("(c p) n -> p c n", p=P)) \
                    .then_inc(w_in, 16)
            sp.wait_ge(wup_zero, 1)
            for i in range(4):
                sp.dma_start(wup[LAT * i:LAT * (i + 1), i, :], (wku_ap, wvu_ap)[i // 2]).then_inc(w_in, 16)
            with sp.Fori(0, NI) as it:
                await_empty(sp, it, "out0")
                await_empty(sp, it, "out1")
                sp.dma_start(o_in[:, :, :, :], o_dram[bass.ds(it * 2, 2)].rearrange("s p h t -> p s h t")) \
                    .then_inc(o_got, 16)
                sp.wait_ge(xn_done, AHEAD + it * 4)
                sp.dma_start(x1[:, :, :], x_ap[bass.ds(it * 2, 2)].rearrange("s t d -> t s d")).then_inc(x_got, 16)

        @block.gpsimd
        def _(pool):
            for count in (xn_done, *copied):
                pool.sem_inc(count, AHEAD)
            pool.memset(wup[:, :, :], 0.0).then_inc(wup_zero, 1)
            pool.memset(mhalf[:, :], -0.5).then_inc(consts, 1)
            pool.memset(one[:, :], 1.0).then_inc(consts, 1)
            pool.memset(ident[:, :], 0.0).then_inc(consts, 1)
            pool.memset(mask[:, :], 0.0).then_inc(consts, 1)
            pool.wait_ge(consts, 4)
            pool.affine_select(out=ident[:, :], in_=ident[:, :], compare_op=ALU.not_equal, fill=1.0, base=0,
                               pattern=[[-1, P]], channel_multiplier=1).then_inc(consts, 1)
            pool.affine_select(out=mask[:, :], in_=mask[:, :], compare_op=ALU.is_ge, fill=-3.0e38, base=0,
                               pattern=[[-1, P]], channel_multiplier=1).then_inc(consts, 1)
            pool.wait_ge(consts, 6)
            pool.wait_ge(w_in, W_IN)

            def rsqrt(it, k, s):
                pool.wait_ge(var_done, it * 4 + (2 * k + s + 1))
                nc.gpsimd.tensor_tensor(rstd[:, k, s, :], rstd[:, k, s, :], mhalf[:, :], ALU.pow) \
                    .then_inc(rstd_done, 1)

            with pool.Fori(0, NI) as it:
                pool.wait_ge(x_got, it * 16 + 16)
                for s in range(2):
                    nc.gpsimd.tensor_tensor(x1[:, s, :], x1[:, s, :], bo[:, :], ALU.add).then_inc(xb_done, 1)
                for s in range(2):
                    rsqrt(it, 0, s)
                for s in range(2):
                    rsqrt(it, 1, s)
                for s in range(2):
                    await_copied(pool, it, f"x3T{s}")
                    toks = bass.ds(it * T2 + s * T, T)
                    nc.gpsimd.tensor_tensor(xT_h[:, :, toks], x3T[:, s],
                                            one[:, :].unsqueeze(2).broadcast_to([P, DC, T]), ALU.mult) \
                        .then_inc(hi_done, 1)
                    pool.wait_ge(hi_done, it * 2 + (s + 1))
                    nc.gpsimd.tensor_tensor(xT_l[:, :, toks], x3T[:, s], xT_h[:, :, toks], ALU.subtract) \
                        .then_inc(lo_done, 1)

        @block.tensor
        def _(pe):
            def accumulate(name, out, pieces, skip=False):
                for c, (w, m) in enumerate(pieces):
                    mm = nc.tensor.matmul(out, w, m, start=(c == 0), stop=(c == len(pieces) - 1))
                return mm

            def fill(mm, name):
                mm.then_inc(filled[place[name][0]], 1)

            pe.wait_ge(consts, 6)
            pe.wait_ge(w_in, W_IN)
            with pe.Fori(0, NI) as it:
                pe.wait_ge(o_got, it * 16 + 16)
                for s in range(2):
                    name = f"out{s}"
                    await_empty(pe, it, name)
                    fill(accumulate(name, bank(name), [(o_in[:, s, p, :], wxo[:, p, :]) for p in range(PAIRS)]), name)
                for s in range(2):
                    name = f"xT{s}"
                    await_empty(pe, it, name)
                    pe.wait_ge(xn_done, AHEAD + it * 4 + (s + 1))
                    for c in range(DC):
                        mm = nc.tensor.transpose(bank(name)[:, c * P:(c + 1) * P], xn[:, s, c * P:(c + 1) * P],
                                                 ident[:, :])
                    fill(mm, name)
                for s in range(2):
                    await_copied(pe, it, f"xT{s}")
                for n in range(SH // 2):
                    name = f"q{n}"
                    await_empty(pe, it, name)
                    for h in (2 * n, 2 * n + 1):
                        mm = accumulate(name, bank(name)[:, (h % 2) * T2:(h % 2 + 1) * T2],
                                        [(wq[:, c, h * SD:(h + 1) * SD], xnT[:, c, :, :]) for c in range(DC)])
                    fill(mm, name)
                await_empty(pe, it, "lat")
                fill(accumulate("lat", bank("lat")[:, 0:T2], [(wdown[:, c, :], xnT[:, c, :, :]) for c in range(DC)]),
                     "lat")
                await_copied(pe, it, "lat")
                await_empty(pe, it, "kT")
                for g in range(SKV):
                    mm = accumulate("kT", bank("kT")[:, g * T2:(g + 1) * T2], [(wup[:, g, :], lat[:, :, :])])
                fill(mm, "kT")
                await_empty(pe, it, "v")
                for s in range(2):
                    mm = accumulate("v", bank("v")[:, s * SKV * SD:(s + 1) * SKV * SD],
                                    [(lat[:, s, :], wup[:, 2:4, :])])
                fill(mm, "v")
                for name in ("q0", "q1", "q2", "q3", "kT"):
                    await_copied(pe, it, name)
                for s in range(2):
                    for g in range(SKV):
                        name = f"sc{s}{g}"
                        await_empty(pe, it, name)
                        for r in range(REP):
                            mm = accumulate(name, bank(name)[:, r * T:(r + 1) * T],
                                            [(qT[:, g * REP + r, s, :], kT[:, g, s, :])])
                        fill(mm, name)
                for s in range(2):
                    for g in range(SKV):
                        name = f"pT{s}{g}"
                        await_empty(pe, it, name)
                        pe.wait_ge(p_done, it * 4 + (2 * s + g + 1))
                        for r in range(REP):
                            mm = nc.tensor.transpose(bank(name)[:, r * T:(r + 1) * T], sm[:, s, g, r, :], ident[:, :])
                        fill(mm, name)
                await_copied(pe, it, "v")
                for s in range(2):
                    for g in range(SKV):
                        name = f"y{s}{g}"
                        await_empty(pe, it, name)
                        await_copied(pe, it, f"pT{s}{g}")
                        fill(accumulate(name, bank(name), [(v[:, s, g, :], pT[:, s, g, :, :])]), name)
                for s in range(2):
                    name = f"wo{s}"
                    await_empty(pe, it, name)
                    for g in range(SKV):
                        await_copied(pe, it, f"y{s}{g}")
                    fill(accumulate(name, bank(name), [(yT[:, s, h, :], wo[:, h, :]) for h in range(SH)]), name)
                for s in range(2):
                    name = f"x3T{s}"
                    await_empty(pe, it, name)
                    pe.wait_ge(xn_done, AHEAD + it * 4 + (2 + s + 1))
                    for c in range(DC):
                        mm = nc.tensor.transpose(bank(name)[:, c * P:(c + 1) * P], xn[:, s, c * P:(c + 1) * P],
                                                 ident[:, :])
                    fill(mm, name)
                for s in range(2):
                    name = f"lg{s}"
                    await_empty(pe, it, name)
                    await_copied(pe, it, f"x3T{s}")
                    fill(accumulate(name, bank(name)[:, 0:E], [(x3T[:, s, c, :], wg[:, c, :]) for c in range(DC)]),
                         name)

        def evacuate(eng, it, name, dst, src, copy):
            await_filled(eng, it, name)
            copy(dst, src).then_inc(copied[place[name][0]], 1)

        @block.scalar
        def _(act):
            def copy(dst, src):
                return nc.scalar.activation(dst, src, ACT.Copy)

            with act.Fori(0, NI) as it:
                for s in range(2):
                    evacuate(act, it, f"xT{s}", xnT[:, :, s, :], bank(f"xT{s}").rearrange("p (c t) -> p c t", c=DC), copy)
                for n in range(2):
                    evacuate(act, it, f"q{n}", qT[:, 2 * n:2 * n + 2].rearrange("p h s t -> p (h s t)"),
                             bank(f"q{n}"), copy)
                evacuate(act, it, "kT", kT[:, :, :, :].rearrange("p g s t -> p (g s t)"), bank("kT"), copy)
                for n in range(4):
                    act.wait_ge(sub_done, it * 4 + (n + 1))
                    t = sm[:, n // 2, n % 2]
                    nc.scalar.activation(t, t, ACT.Exp).then_inc(exp_done, 1)
                for s in range(2):
                    for g in range(SKV):
                        evacuate(act, it, f"pT{s}{g}", pT[:, s, g].rearrange("p r t -> p (r t)"),
                                 bank(f"pT{s}{g}"), copy)
                    if s:
                        for g in range(SKV):
                            evacuate(act, it, f"y0{g}", yT[:, 0, g * REP:(g + 1) * REP].rearrange("p r t -> p (r t)"),
                                     bank(f"y0{g}"), copy)
                for s in range(2):
                    evacuate(act, it, f"x3T{s}", x3T[:, s].rearrange("p c t -> p (c t)"), bank(f"x3T{s}"), copy)

        @block.vector
        def _(dve):
            STEPS = 2 * 4 + 4 + 2 * 4 + 2

            with dve.Fori(0, NI) as it:
                steps = [0]

                def link(ins):
                    steps[0] += 1
                    ins.then_inc(dve_step, 1)
                    dve.wait_ge(dve_step, it * STEPS + steps[0])

                def norm_stats(k, s, x):
                    link(nc.vector.bn_stats(stats[:, k, s, :], x))
                    nc.vector.memset(hold[:, k, s, :], 0.0)
                    link(nc.vector.bn_aggr(mv[:, k, s, :], stats[:, k, s, :]))
                    nc.vector.tensor_scalar(rstd[:, k, s, :], mv[:, k, s, 1:2], EPS, None, ALU.add) \
                        .then_inc(var_done, 1)

                def norm(k, s, x):
                    dve.wait_ge(rstd_done, it * 4 + (2 * k + s + 1))
                    nc.vector.tensor_scalar(xn[:, s, :], x, mv[:, k, s, 0:1], rstd[:, k, s, :],
                                            ALU.subtract, ALU.mult).then_inc(xn_done, 1)

                for s in range(2):
                    dve.wait_ge(xb_done, it * 2 + (s + 1))
                    await_filled(dve, it, f"out{s}")
                    i, n = place[f"out{s}"]
                    nc.vector.tensor_tensor(x1[:, s, :], bank(f"out{s}"), x1[:, s, :], ALU.add).then_inc(copied[i], 1)
                    await_copied(dve, it, f"out{s}")
                    norm_stats(0, s, x1[:, s, :])
                for s in range(2):
                    norm(0, s, x1[:, s, :])
                for n in range(2, 4):
                    evacuate(dve, it, f"q{n}", qT[:, 2 * n:2 * n + 2].rearrange("p h s t -> p (h s t)"),
                             bank(f"q{n}"), nc.vector.tensor_copy)
                evacuate(dve, it, "lat", lat[:, :, :].rearrange("p s t -> p (s t)"), bank("lat")[:, 0:T2],
                         nc.vector.tensor_copy)
                evacuate(dve, it, "v", v[:, :, :, :].rearrange("p s g d -> p (s g d)"), bank("v"),
                         nc.vector.tensor_copy)
                for s in range(2):
                    for g in range(SKV):
                        name = f"sc{s}{g}"
                        await_filled(dve, it, name)
                        t = sm[:, s, g]
                        nc.vector.scalar_tensor_tensor(
                            out=t, in0=bank(name).rearrange("p (r t) -> p r t", r=REP), scalar=S_SCALE,
                            in1=mask[:, :].unsqueeze(1).broadcast_to([P, REP, T]), op0=ALU.mult, op1=ALU.add) \
                            .then_inc(copied[place[name][0]], 1)
                        await_copied(dve, it, name)
                        link(nc.vector.tensor_reduce(mx[:, s, g, :], t, AX_X, ALU.max))
                        nc.vector.tensor_tensor(t, t, mx[:, s, g, :].unsqueeze(2).broadcast_to([P, REP, T]),
                                                ALU.subtract).then_inc(sub_done, 1)
                for s in range(2):
                    for g in range(SKV):
                        dve.wait_ge(exp_done, it * 4 + (2 * s + g + 1))
                        t = sm[:, s, g]
                        link(nc.vector.tensor_reduce(sums[:, s, g, :], t, AX_X, ALU.add))
                        link(nc.vector.reciprocal(inv[:, s, g, :], sums[:, s, g, :]))
                        nc.vector.tensor_tensor(t, t, inv[:, s, g, :].unsqueeze(2).broadcast_to([P, REP, T]),
                                                ALU.mult).then_inc(p_done, 1)
                for g in range(SKV):
                    evacuate(dve, it, f"y1{g}", yT[:, 1, g * REP:(g + 1) * REP].rearrange("p r t -> p (r t)"),
                             bank(f"y1{g}"), nc.vector.tensor_copy)
                for s in range(2):
                    await_filled(dve, it, f"wo{s}")
                    x2s = x2[:, bass.ds(it * 2 + s, 1), :].rearrange("p o d -> p (o d)")
                    nc.vector.tensor_tensor(x1[:, s, :], bank(f"wo{s}"), x1[:, s, :], ALU.add) \
                        .then_inc(copied[place[f"wo{s}"][0]], 1)
                    await_copied(dve, it, f"wo{s}")
                    link(nc.vector.tensor_copy(x2s, x1[:, s, :]))
                    norm_stats(1, s, x1[:, s, :])
                for s in range(2):
                    norm(1, s, x1[:, s, :])
                for s in range(2):
                    evacuate(dve, it, f"lg{s}", logits[:, bass.ds(it * 2 + s, 1), :].rearrange("p o e -> p (o e)"),
                             bank(f"lg{s}")[:, 0:E], nc.vector.tensor_copy)
                assert steps[0] == STEPS, steps



def experts(nc, up_ap, down_ap, out_ap, x2, xT_h, xT_l, logits):
    with ExitStack() as ctx:
        def sb(name, shape, dt=F32):
            return ctx.enter_context(nc.sbuf_tensor(name, shape, dt))

        def sem(name):
            return ctx.enter_context(nc.semaphore(name))

        NE = E + 1
        FC = F // P
        NT = B * T // P
        HTOK = B * T // 2
        NS = 4
        wu = sb("wu", [P, 2, DC, F], F32R)
        wd = sb("wd", [P, 2, FC, D], F32R)
        stage = sb("stage3", [P, NS, F])
        g_h = sb("g_h", [P, FC, HTOK], F32R)
        g_l = sb("g_l", [P, FC, HTOK], F32R)
        gf = sb("gf", [P, 4, HTOK])
        iota = sb("iota", [P, E])
        probs = sb("probs3", [P, NT, E])
        lmax = sb("lmax", [P, NT])
        den = sb("den", [P, NT])
        rden = sb("rden3", [P, NT])
        top = sb("top", [P, NT, 8])
        index = sb("index", [P, NT, 8], U32)
        index_f = sb("index_f", [P, NT, 2])
        weight = sb("weight", [P, NT, 2])
        hit = sb("hit", [P, 2, NT, E])
        cw = sb("cw", [P, NE, NT])
        up_ps = ctx.enter_context(nc.psum_tensor("up_ps", [P, 4, 512], F32))
        down_ps = ctx.enter_context(nc.psum_tensor("down_ps", [P, 4, 512], F32))

        raw_in = [sem(f"raw3_in{i}") for i in range(NS)]
        w_hi = sem("w_hi")
        w_lo = sem("w_lo")
        up_done = sem("up_done")
        gelu_done = sem("gelu_done")
        g_hi = sem("g_hi")
        g_lo = sem("g_lo")
        down_done = sem("down_done")
        acc_done = sem("acc_done")
        iota_done = sem("iota_done")
        route = sem("route")
        e_done = sem("e_done")
        out_stored = sem("out_stored")

        PIECES = 8
        block = ctx.enter_context(nc.Block())

        @block.sync
        def _(sp):
            with sp.Fori(0, NE) as e:
                for i in range(PIECES):
                    sp.wait_ge(w_lo, e * PIECES + (i + 1))
                    if i < 4:
                        src = up_ap[bass.ds(e, 1), i * P:(i + 1) * P, :].rearrange("o p n -> (o p) n")
                        dst = stage[:, i % NS, :]
                    else:
                        src = down_ap[bass.ds(e, 1), 2 * (i - 4) * P:2 * (i - 3) * P, :] \
                            .rearrange("o (c p) n -> (o p) c n", p=P)
                        dst = stage[:, i % NS, :].rearrange("p (c n) -> p c n", c=2)
                    sp.dma_start(dst, src).then_inc(raw_in[i % NS], 16)
            for t in range(NT):
                sp.wait_ge(acc_done, AHEAD + E * NT + t + 1)
                sp.dma_start(out_ap[t], x2[:, t, :]).then_inc(out_stored, 16)
            sp.wait_ge(out_stored, 16 * NT)

        def halves(i):
            if i < 4:
                return wu[:, 0, i, :], wu[:, 1, i, :]
            return tuple(wd[:, k, 2 * (i - 4):2 * (i - 3), :].rearrange("p c n -> p (c n)") for k in range(2))

        @block.gpsimd
        def _(pool):
            for count in (up_done, gelu_done, g_lo, down_done, acc_done):
                pool.sem_inc(count, AHEAD)
            pool.sem_inc(w_lo, NS)
            pool.iota(iota[:, :], pattern=[[1, E]], base=0, channel_multiplier=0,
                      allow_small_or_imprecise_dtypes=True).then_inc(iota_done, 1)
            pool.memset(cw[:, 0, :], 1.0).then_inc(iota_done, 1)
            with pool.Fori(0, NE) as e:
                for i in range(PIECES):
                    hi, lo = halves(i)
                    pool.wait_ge(w_hi, e * PIECES + (i + 1))
                    nc.gpsimd.tensor_tensor(lo, stage[:, i % NS, :], hi, ALU.subtract).then_inc(w_lo, 1)

        @block.tensor
        def _(pe):
            with pe.Fori(0, NE) as e:
                for half in range(2):
                    toks = slice(half * HTOK, (half + 1) * HTOK)
                    for f in range(FC):
                        if half == 0 and f == 0:
                            pe.wait_ge(w_lo, e * PIECES + (NS + 4))
                        pe.wait_ge(gelu_done, AHEAD + e * (2 * FC) + max(FC * half + f - 3, 0))
                        cols = slice(f * P, (f + 1) * P)
                        for c in range(DC):
                            for k, (w, m) in enumerate(((0, xT_h), (0, xT_l), (1, xT_h))):
                                mm = nc.tensor.matmul(up_ps[:, f % 4, :], wu[:, w, c, cols], m[:, c, toks],
                                                      start=(c + k == 0), stop=(c == DC - 1 and k == 2))
                        mm.then_inc(up_done, 1)
                    for t in range(4):
                        pe.wait_ge(acc_done, AHEAD + e * NT + (4 * (half - 1) + t + 1 if half else 0))
                        rows = slice(t * P, (t + 1) * P)
                        for f in range(FC):
                            if t == 0:
                                pe.wait_ge(g_lo, AHEAD + e * (2 * FC) + (FC * half + f + 1))
                                if half == 0 and f % 2 == 0:
                                    pe.wait_ge(w_lo, e * PIECES + (NS + 4 + f // 2 + 1))
                            for k, (g, w) in enumerate(((g_h, 0), (g_h, 1), (g_l, 0))):
                                mm = nc.tensor.matmul(down_ps[:, t, :], g[:, f, rows], wd[:, w, f, :],
                                                      start=(f + k == 0), stop=(f == FC - 1 and k == 2))
                        mm.then_inc(down_done, 1)

        @block.scalar
        def _(act):
            def split_hi(e, i):
                act.wait_ge(raw_in[i % NS], e * (16 * PIECES // NS) + 16 * (i // NS + 1))
                hi, _ = halves(i)
                nc.scalar.activation(hi, stage[:, i % NS, :], ACT.Copy).then_inc(w_hi, 1)

            act.wait_ge(route, 2)
            nc.scalar.activation(probs[:, :, :], probs[:, :, :], ACT.Exp).then_inc(e_done, 1)
            with act.Fori(0, NE) as e:
                act.wait_ge(up_done, AHEAD + e * (2 * FC))
                for i in range(4):
                    split_hi(e, i)
                act.wait_ge(down_done, AHEAD + e * NT)
                for half in range(2):
                    for f in range(FC):
                        if half == 0 and f < 4:
                            split_hi(e, 4 + f)
                        act.wait_ge(up_done, AHEAD + e * (2 * FC) + (FC * half + f + 1))
                        act.wait_ge(g_lo, AHEAD + e * (2 * FC) + max(FC * half + f - 3, 0))
                        nc.scalar.activation(gf[:, f % 4, :], up_ps[:, f % 4, :], ACT.Gelu).then_inc(gelu_done, 1)

        @block.vector
        def _(dve):
            steps = [0]

            def link(ins):
                steps[0] += 1
                ins.then_inc(route, 1)
                dve.wait_ge(route, steps[0])

            link(nc.vector.tensor_reduce(lmax[:, :], logits[:, :, :], AX_X, ALU.max))
            link(nc.vector.tensor_tensor(probs[:, :, :], logits[:, :, :], lmax[:, :].unsqueeze(2)
                                         .broadcast_to([P, NT, E]), ALU.subtract))
            dve.wait_ge(e_done, 1)
            link(nc.vector.tensor_reduce(den[:, :], probs[:, :, :], AX_X, ALU.add))
            link(nc.vector.reciprocal(rden[:, :], den[:, :]))
            link(nc.vector.tensor_tensor(probs[:, :, :], probs[:, :, :], rden[:, :].unsqueeze(2)
                                         .broadcast_to([P, NT, E]), ALU.mult))
            for t in range(NT):
                link(nc.vector.max(top[:, t, :], probs[:, t, :]))
                link(nc.vector.max_index(index[:, t, :], top[:, t, :], probs[:, t, :]))
            link(nc.vector.tensor_copy(index_f[:, :, :], index[:, :, 0:2]))
            link(nc.vector.tensor_tensor(den[:, :], top[:, :, 0], top[:, :, 1], ALU.add))
            link(nc.vector.reciprocal(rden[:, :], den[:, :]))
            link(nc.vector.tensor_tensor(weight[:, :, :], top[:, :, 0:2], rden[:, :].unsqueeze(2)
                                         .broadcast_to([P, NT, 2]), ALU.mult))
            dve.wait_ge(iota_done, 2)
            for k in range(2):
                link(nc.vector.tensor_tensor(hit[:, k], iota[:, :].unsqueeze(1).broadcast_to([P, NT, E]),
                                             index_f[:, :, k:k + 1].broadcast_to([P, NT, E]), ALU.is_equal))
                link(nc.vector.tensor_tensor(hit[:, k], hit[:, k],
                                             weight[:, :, k:k + 1].broadcast_to([P, NT, E]), ALU.mult))
            link(nc.vector.tensor_tensor(cw[:, 1:NE, :].rearrange("p e t -> p t e"), hit[:, 0], hit[:, 1], ALU.add))

            with dve.Fori(0, NE) as e:
                for half in range(2):
                    dve.wait_ge(down_done, AHEAD + e * NT + 4 * half)
                    for f in range(FC):
                        n = FC * half + f
                        dve.wait_ge(gelu_done, AHEAD + e * (2 * FC) + (n + 1))
                        nc.vector.tensor_copy(g_h[:, f, :], gf[:, f % 4, :]).then_inc(g_hi, 1)
                        dve.wait_ge(g_hi, e * (2 * FC) + (n + 1))
                        nc.vector.tensor_tensor(g_l[:, f, :], gf[:, f % 4, :], g_h[:, f, :], ALU.subtract) \
                            .then_inc(g_lo, 1)
                    for t in range(4):
                        n = 4 * half + t
                        dve.wait_ge(down_done, AHEAD + e * NT + (n + 1))
                        dve.wait_ge(acc_done, AHEAD + e * NT)
                        nc.vector.scalar_tensor_tensor(
                            out=x2[:, n, :], in0=down_ps[:, t, :],
                            scalar=cw[:, bass.ds(e, 1), n:n + 1].rearrange("p o t -> p (o t)"),
                            in1=x2[:, n, :], op0=ALU.mult, op1=ALU.add).then_inc(acc_done, 1)


def perceiver_block(nc, x, ctx_t, xq, xk, xv, xo, xbo, sq, skd, svd, sku, svu, so, gate, up, down, out):
    q_dram = nc.dram_tensor("q_scratch", (2, PAIRS, P, B * T), F32, kind="Internal").ap()
    o_dram = nc.dram_tensor("o_scratch", (B, P, PAIRS, T), F32, kind="Internal").ap()
    cross_attention(nc, x, ctx_t, xq, xk, xv, q_dram, o_dram)
    with ExitStack() as ctx:
        x2 = ctx.enter_context(nc.sbuf_tensor("x2", [P, B, D], F32))
        xT_h = ctx.enter_context(nc.sbuf_tensor("xT_h", [P, DC, B * T], F32R))
        xT_l = ctx.enter_context(nc.sbuf_tensor("xT_l", [P, DC, B * T], F32R))
        logits = ctx.enter_context(nc.sbuf_tensor("logits", [P, B, E], F32))
        self_attention(nc, x, xbo, xo, sq, skd, svd, sku, svu, so, gate, o_dram, x2, xT_h, xT_l, logits)
        experts(nc, up, down, out, x2, xT_h, xT_l, logits)


def kernel(**inputs):
    import numpy as _np
    import concourse.bacc as _bacc
    from concourse import mybir as _mybir
    from concourse.bass_utils import run_bass_kernel_spmd as _run

    a = {k: _np.asarray(v) for k, v in inputs.items()}
    ctx_t = a["ctx_1024"].reshape(B, NQ, QT, DC, P).transpose(0, 1, 4, 3, 2)
    laid = [
        ("x", a["x"]), ("ctx", ctx_t), ("xq", a["L0_xattn_Wq"]), ("xk", a["L0_xattn_Wk"]),
        ("xv", a["L0_xattn_Wv"]), ("xo", a["L0_xattn_Wo"]), ("xbo", a["L0_xattn_bo"]),
        ("sq", a["L0_attn_wq"]), ("skd", a["L0_attn_wk_down"]), ("svd", a["L0_attn_wv_down"]),
        ("sku", a["L0_attn_wk_up"]), ("svu", a["L0_attn_wv_up"]), ("so", a["L0_attn_wo"]),
        ("gate", a["L0_ffn_Wg"]),
        ("up", _np.concatenate([a["L0_ffn_W1"][None], a["L0_ffn_Wu"]])),
        ("down", _np.concatenate([a["L0_ffn_W2"][None], a["L0_ffn_Wd"]])),
    ]
    nc = _bacc.Bacc("TRN2", target_bir_lowering=False, num_devices=1, dynamic_dma_scratch_size=1024)
    arrays, args = {}, []
    for name, v in laid:
        v = _np.ascontiguousarray(v)
        arrays[f"in_{name}_dram"] = v
        args.append(nc.dram_tensor(f"in_{name}_dram", v.shape, _mybir.dt.from_np(v.dtype), kind="ExternalInput").ap())
    args.append(nc.dram_tensor("out_0_dram", (B, T, D), _mybir.dt.float32, kind="ExternalOutput").ap())
    perceiver_block(nc, *args)
    r = _run(nc, [arrays], core_ids=[0])
    return r.results[0]["out_0_dram"]
```

```python
from contextlib import ExitStack

import concourse.bass as bass
from concourse import mybir

F32 = mybir.dt.float32
F32R = mybir.dt.float32r
U32 = mybir.dt.uint32
ALU = mybir.AluOpType
ACT = mybir.ActivationFunctionType
AX_X = mybir.AxisListType.X

P = 128
EPS = 1e-5

B, T, D = 8, 128, 512
M = 2048
XH, XD = 8, 64
SH, SKV, SD, LAT = 8, 2, 128, 32
REP = SH // SKV
E, F = 8, 1024
MAX_TILES = B * T // P + (2 * B * T - E) // P + E
DC = D // P
PAIRS = XH // 2
QT = 512
NQ = M // QT
MT = M // P
X_SCALE = XD ** -0.5
S_SCALE = SD ** -0.5

AHEAD = 1


def cross_attention(nc, x_ap, ctx_ap, wq_ap, wk_ap, wv_ap, q_dram, o_dram, rows_dram):
    with ExitStack() as ctx:
        def sb(name, shape, dt):
            return ctx.enter_context(nc.sbuf_tensor(name, shape, dt))

        def sem(name):
            return ctx.enter_context(nc.semaphore(name))

        wk = sb("wk", [P, 2, DC, D], F32R)
        wv = sb("wv", [P, 2, DC, D], F32R)
        stage = sb("stage", [P, 2, 2, QT], F32)
        ctx_h = sb("ctx_h", [P, 2, DC, QT], F32R)
        ctx_l = sb("ctx_l", [P, 2, DC, QT], F32R)
        kT = sb("kT", [P, 2, PAIRS, M], F32R)
        vt = sb("vt", [P, MT, D], F32)
        qa = sb("qa", [P, XH, T], F32R)
        qb = sb("qb", [P, XH, T], F32R)
        probs = sb("probs", [P, 2, M], F32)
        pT = sb("pT", [P, 2, MT, P], F32)
        on = sb("on", [P, PAIRS, P], F32)
        ident = sb("ident", [P, P], F32)
        one = sb("one", [P, 1], F32)
        zero = sb("zero", [P, D], F32)
        mhalf = sb("mhalf", [P, 1], F32)
        spread = sb("spread", [P, XH, XD], F32)
        smax = sb("smax", [P, XH, 2], F32)
        nmax = sb("nmax", [P, XH], F32)
        rsum = sb("rsum", [P, XH, 2], F32)
        rtot = sb("rtot", [P, XH], F32)
        rinv = sb("rinv", [P, XH], F32)
        stats = sb("stats", [P, B, 6], F32)
        mv = sb("mv", [P, B, 2], F32)
        rstd = sb("rstd", [P, B], F32)

        x_all = probs[:, :, :].rearrange("p a (b d) -> p (a b) d", d=D)
        pT_flat = pT[:, :, :, :].rearrange("p a t m -> p a (t m)")
        wq = pT_flat[:, 0, :].rearrange("p (c n) -> p c n", c=DC)
        xnT = pT_flat[:, 1, :].rearrange("p (c n) -> p c n", c=DC)
        qa_flat = qa[:, :, :].rearrange("p (s h) t -> p s (h t)", s=2)
        qb_flat = qb[:, :, :].rearrange("p (s h) t -> p s (h t)", s=2)

        ps_s = ctx.enter_context(nc.psum_tensor("ps_s", [P, 4, 512], F32))
        ps_t = ctx.enter_context(nc.psum_tensor("ps_t", [P, 2, 4, P], F32))
        ps_o = ctx.enter_context(nc.psum_tensor("ps_o", [P, PAIRS, P], F32))
        ps_r = ctx.enter_context(nc.psum_tensor("ps_r", [P, PAIRS, P], F32))

        x_in = sem("x_in")
        wq_in = sem("wq_in")
        ident_ok = sem("ident_ok")
        zero_ok = sem("zero_ok")
        zeroed = sem("zeroed")
        bn_done = sem("bn_done")
        rstd_done = sem("rstd_done")
        xn_done = sem("xn_done")
        xT_done = sem("xT_done")
        xT_copied = sem("xT_copied")
        qp_done = sem("qp_done")
        q_hi = sem("q_hi")
        q_lo = sem("q_lo")
        q_stored = [sem("q_stored0"), sem("q_stored1")]
        raw_in = [sem("raw_in0"), sem("raw_in1")]
        hi_done = sem("hi_done")
        split_done = sem("split_done")
        proj_done = sem("proj_done")
        k_hi = sem("k_hi")
        k_lo = sem("k_lo")
        v_copied = sem("v_copied")
        q_in = sem("q_in")
        s_done = sem("s_done")
        max_done = sem("max_done")
        nmax_done = sem("nmax_done")
        exp_done = sem("exp_done")
        t_done = sem("t_done")
        pT_even = sem("pT_even")
        pT_odd = sem("pT_odd")
        pv_done = sem("pv_done")
        sum_done = sem("sum_done")
        spread_done = sem("spread_done")
        r_done = sem("r_done")
        r_copied = sem("r_copied")
        on_done = sem("on_done")
        o_stored = sem("o_stored")

        HB = B // 2
        HT = HB * T
        NW = 2 * DC // 2
        LB = NQ * DC // 2
        GQ = PAIRS + QT // P
        GB = NQ * GQ

        block = ctx.enter_context(nc.Block())

        @block.sync
        def _(sp):
            sp.dma_start(x_all, x_ap.rearrange("b t d -> t b d")).then_inc(x_in, 16)
            sp.dma_start(wq, wq_ap.rearrange("(c p) n -> p c n", p=P)).then_inc(wq_in, 16)
            for n in range(NW):
                w_ap, c = (wk_ap, wv_ap)[n // 2], 2 * (n % 2)
                if n >= 2:
                    sp.wait_ge(split_done, n - 1)
                sp.dma_start(stage[:, n % 2], w_ap[c * P:(c + 2) * P, :].rearrange("(c p) n -> p c n", p=P)) \
                    .then_inc(raw_in[n % 2], 16)
            sp.wait_ge(zero_ok, 1)
            for n in range(B * T // P, MAX_TILES + 1):
                sp.dma_start(rows_dram[n], zero[:, :]).then_inc(zeroed, 16)
            with sp.Fori(0, B) as b:
                for k in range(LB):
                    sp.wait_ge(split_done, b * LB + (NW + k - 1))
                    sp.dma_start(stage[:, k % 2],
                                 ctx_ap[bass.ds(b, 1), k // 2, :, 2 * (k % 2):2 * (k % 2) + 2, :]
                                 .rearrange("o p c m -> (o p) c m")).then_inc(raw_in[k % 2], 16)
            sp.wait_ge(zeroed, 16 * (MAX_TILES + 1 - B * T // P))

        @block.gpsimd
        def _(pool):
            for count in (s_done, exp_done, pT_even, pT_odd, on_done, o_stored):
                pool.sem_inc(count, AHEAD)
            pool.memset(zero[:, :], 0.0).then_inc(zero_ok, 1)
            pool.memset(one[:, :], 1.0).then_inc(ident_ok, 1)
            pool.memset(mhalf[:, :], -0.5).then_inc(ident_ok, 1)
            pool.memset(ident[:, :], 0.0).then_inc(ident_ok, 1)
            pool.wait_ge(ident_ok, 3)
            pool.affine_select(out=ident[:, :], in_=ident[:, :], compare_op=ALU.not_equal, fill=1.0, base=0,
                               pattern=[[-1, P]], channel_multiplier=1).then_inc(ident_ok, 1)
            pool.wait_ge(ident_ok, 4)

            def split(hi, lo, slot, loads, before):
                pool.wait_ge(raw_in[slot], loads)
                nc.gpsimd.tensor_tensor(hi, stage[:, slot], one[:, 0:1].unsqueeze(2).broadcast_to([P, 2, QT]),
                                        ALU.mult).then_inc(hi_done, 1)
                pool.wait_ge(hi_done, before + 1)
                nc.gpsimd.tensor_tensor(lo, stage[:, slot], hi, ALU.subtract).then_inc(split_done, 1)

            for n in range(NW):
                w, c = (wk, wv)[n // 2], 2 * (n % 2)
                split(w[:, 0, c:c + 2, :], w[:, 1, c:c + 2, :], n % 2, 16 * (n // 2 + 1), n)
                if n == 0:
                    pool.wait_ge(bn_done, 2 * B + 1)
                    nc.gpsimd.tensor_tensor(rstd[:, :], rstd[:, :], mhalf[:, :].broadcast_to([P, B]), ALU.pow) \
                        .then_inc(rstd_done, 1)
            with pool.Fori(0, B) as b:
                for k in range(LB):
                    g, c = k // 2, 2 * (k % 2)
                    if c == 0:
                        pool.wait_ge(proj_done, b * GB + GQ * (g + 1))
                    split(ctx_h[:, g % 2, c:c + 2, :], ctx_l[:, g % 2, c:c + 2, :], k % 2,
                          b * (16 * LB // 2) + 16 * (NW // 2 + k // 2 + 1), b * LB + (NW + k))

        @block.tensor
        def _(pe):
            pe.wait_ge(ident_ok, 4)
            for half in range(2):
                for i in range(HB):
                    n = half * HB + i
                    pe.wait_ge(xn_done, n + 1)
                    if n >= 2:
                        pe.wait_ge(xT_copied, n - 1)
                    for c in range(DC):
                        last = nc.tensor.transpose(ps_t[:, n % 2, c, :], x_all[:, n, c * P:(c + 1) * P], ident[:, :])
                    last.then_inc(xT_done, 1)
                pe.wait_ge(wq_in, 16)
                pe.wait_ge(xT_copied, (half + 1) * HB)
                for p in range(PAIRS):
                    if half:
                        pe.wait_ge(q_lo, p + 1)
                    for c in range(DC):
                        last = nc.tensor.matmul(ps_s[:, p, :], wq[:, c, p * P:(p + 1) * P], xnT[:, c, :],
                                                start=(c == 0), stop=(c == DC - 1))
                    last.then_inc(qp_done, 1)
            pe.wait_ge(q_lo, 2 * PAIRS)

            def three(out, w_hi, w_lo, m_hi, m_lo):
                for c in range(DC):
                    for k, (w, m) in enumerate(((w_hi, m_hi), (w_hi, m_lo), (w_lo, m_hi))):
                        mm = nc.tensor.matmul(out, w(c), m(c), start=(c + k == 0), stop=(c == DC - 1 and k == 2))
                return mm

            with pe.Fori(0, B) as b:
                pe.wait_ge(exp_done, AHEAD + b * (2 * XH))
                for g in range(NQ):
                    pe.wait_ge(split_done, b * LB + (NW + 2 * (g + 1)))
                    h, l = ctx_h[:, g % 2], ctx_l[:, g % 2]
                    for p in range(PAIRS):
                        if g:
                            pe.wait_ge(v_copied, b * MT + (4 * (g - 1) + p + 1))
                        cols = slice(p * P, (p + 1) * P)
                        three(ps_s[:, p, :], lambda c: wk[:, 0, c, cols], lambda c: wk[:, 1, c, cols],
                              lambda c: h[:, c, :], lambda c: l[:, c, :]).then_inc(proj_done, 1)
                    for t in range(4):
                        pe.wait_ge(k_lo, b * (NQ * PAIRS) + (PAIRS * g + t + 1))
                        rows = slice(t * P, (t + 1) * P)
                        mm = three(ps_s[:, t, :], lambda c: h[:, c, rows], lambda c: l[:, c, rows],
                                   lambda c: wv[:, 0, c, :], lambda c: wv[:, 1, c, :])
                        mm.then_inc(proj_done, 1)

                def scores(h):
                    for j in range(4):
                        if h:
                            pe.wait_ge(exp_done, AHEAD + b * (2 * XH) + (2 * (h - 1) + j // 2 + 1))
                        keys = kT[:, h % 2, h // 2, j * 512:(j + 1) * 512]
                        nc.tensor.matmul(ps_s[:, j, :], qa[:, h, :], keys, start=True, stop=False)
                        mm = nc.tensor.matmul(ps_s[:, j, :], qb[:, h, :], keys, start=False, stop=True)
                        if j % 2:
                            mm.then_inc(s_done, 1)

                def transposes(h):
                    p, e = h // 2, h % 2
                    for j in range(4):
                        if j % 2 == 0:
                            pe.wait_ge(exp_done, AHEAD + b * (2 * XH) + (2 * h + j // 2 + 1))
                        own, other = (pT_odd, pT_even) if e else (pT_even, pT_odd)
                        if j >= 2:
                            pe.wait_ge(own, AHEAD + b * MT + (4 * p + j - 1))
                        else:
                            pe.wait_ge(other, AHEAD + b * MT + (4 * p + j + 3 if e else max(4 * p + j - 1, 0)))
                        for i in range(4):
                            mm = nc.tensor.transpose(ps_t[:, j % 2, i, :],
                                                     probs[:, e, (4 * j + i) * P:(4 * j + i + 1) * P], ident[:, :])
                        mm.then_inc(t_done, 1)

                def values(p, part):
                    if p == 0 and part == 0:
                        pe.wait_ge(on_done, AHEAD + b)
                        pe.wait_ge(v_copied, (b + 1) * MT)
                    pe.wait_ge(pT_even, AHEAD + b * MT + (4 * p + 2 * (part + 1)))
                    pe.wait_ge(pT_odd, AHEAD + b * MT + (4 * p + 2 * (part + 1)))
                    for t in range(8 * part, 8 * part + 8):
                        for e in range(2):
                            h = 2 * p + e
                            mm = nc.tensor.matmul(ps_o[e * XD:(e + 1) * XD, p, :], vt[:, t, h * XD:(h + 1) * XD],
                                                  pT[:, e, t, :], start=(t == 0), stop=(t == MT - 1))
                    return mm

                pe.wait_ge(k_lo, (b + 1) * (NQ * PAIRS))
                pe.wait_ge(v_copied, (b + 1) * MT)
                pe.wait_ge(q_in, (b + 1) * (16 * 8))
                for p in range(PAIRS):
                    scores(2 * p)
                    if p:
                        transposes(2 * p - 1)
                        values(p - 1, 0)
                    scores(2 * p + 1)
                    if p:
                        values(p - 1, 1)
                    transposes(2 * p)
                transposes(XH - 1)
                values(PAIRS - 1, 0)
                values(PAIRS - 1, 1).then_inc(pv_done, 1)
                pe.wait_ge(spread_done, b + 1)
                for p in range(PAIRS):
                    mm = nc.tensor.matmul(ps_r[:, p, :], spread[:, 2 * p:2 * p + 2, :].rearrange("p h d -> p (h d)"),
                                          ident[:, :], start=True, stop=True)
                mm.then_inc(r_done, 1)

        @block.scalar
        def _(act):
            act.sem_inc(proj_done, 2 * GQ)
            for n in range(2 * PAIRS):
                act.wait_ge(qp_done, n + 1)
                if n >= 2:
                    act.wait_ge(q_stored[n % 2], 16 * 2 * (n // 2))
                nc.scalar.activation(qa_flat[:, n % 2, :], ps_s[:, n % PAIRS, :], ACT.Copy).then_inc(q_hi, 1)
                act.wait_ge(q_lo, n + 1)
                half, p = n // PAIRS, n % PAIRS
                for w, src in enumerate((qa_flat, qb_flat)):
                    act.dma_start(q_dram[w, p, :, half * HT:(half + 1) * HT], src[:, n % 2, :].bitcast(F32)) \
                        .then_inc(q_stored[n % 2], 16)
            for done in q_stored:
                act.wait_ge(done, 16 * 2 * PAIRS)
            with act.Fori(0, B) as b:
                act.wait_ge(s_done, AHEAD + b * (2 * XH))
                for w, dst in enumerate((qa, qb)):
                    d = dst[:, :, :].bitcast(F32).rearrange("p (h e) t -> p h e t", e=2)
                    for e in range(2):
                        for to in range(2):
                            act.dma_start(d[to * XD:(to + 1) * XD, :, e, :],
                                          q_dram[w, :, e * XD:(e + 1) * XD, bass.ds(b * T, T)]
                                          .rearrange("h p t -> p h t")).then_inc(q_in, 16)
                for g in range(NQ):
                    keys = slice(g * QT, (g + 1) * QT)
                    for p in range(PAIRS):
                        act.wait_ge(proj_done, b * GB + (GQ * (g + 2) + p + 1))
                        nc.scalar.activation(kT[0:XD, 0, p, keys], ps_s[0:XD, p, :], ACT.Copy)
                        nc.scalar.activation(kT[XD:P, 1, p, keys], ps_s[XD:P, p, :], ACT.Copy).then_inc(k_hi, 1)
                    for t in range(4):
                        act.wait_ge(proj_done, b * GB + (GQ * (g + 2) + PAIRS + t + 1))
                        nc.scalar.activation(vt[:, 4 * g + t, :], ps_s[:, t, :], ACT.Copy).then_inc(v_copied, 1)

                def copy_odd(p):
                    for j in range(4):
                        act.wait_ge(t_done, b * (4 * XH) + (4 * (2 * p + 1) + j + 1))
                        nc.scalar.activation(pT[:, 1, 4 * j:4 * j + 4, :], ps_t[:, j % 2, :, :], ACT.Copy) \
                            .then_inc(pT_odd, 1)

                def exps(h):
                    act.wait_ge(nmax_done, b * XH + (h + 1))
                    for j in range(2):
                        nc.scalar.activation(probs[:, h % 2, j * 1024:(j + 1) * 1024], ps_s[:, 2 * j:2 * j + 2, :],
                                             ACT.Exp, bias=nmax[:, h:h + 1], scale=X_SCALE,
                                             accum_out=rsum[:, h, j:j + 1]).then_inc(exp_done, 1)

                for p in range(PAIRS):
                    if p:
                        copy_odd(p - 1)
                    exps(2 * p)
                    exps(2 * p + 1)
                copy_odd(PAIRS - 1)
                act.wait_ge(on_done, AHEAD + b + 1)
                act.dma_start(o_dram[bass.ds(b, 1)].rearrange("o p h t -> (o p) h t"), on[:, :, :]) \
                    .then_inc(o_stored, 16)
            act.wait_ge(o_stored, AHEAD + 16 * B)

        @block.vector
        def _(dve):
            dve.wait_ge(x_in, 16)
            for n in range(B):
                nc.vector.bn_stats(stats[:, n, :], x_all[:, n, :]).then_inc(bn_done, 1)
            for n in range(B):
                dve.wait_ge(bn_done, n + 1)
                nc.vector.bn_aggr(mv[:, n, :], stats[:, n, :]).then_inc(bn_done, 1)
            dve.wait_ge(bn_done, 2 * B)
            nc.vector.tensor_scalar(rstd[:, :], mv[:, :, 1], EPS, None, ALU.add).then_inc(bn_done, 1)
            dve.wait_ge(rstd_done, 1)
            for n in range(B):
                nc.vector.tensor_scalar(x_all[:, n, :], x_all[:, n, :], mv[:, n, 0:1], rstd[:, n:n + 1],
                                        ALU.subtract, ALU.mult).then_inc(xn_done, 1)

            def q_low(n):
                dve.wait_ge(q_hi, n + 1)
                nc.vector.tensor_tensor(qb_flat[:, n % 2, :], ps_s[:, n % PAIRS, :], qa_flat[:, n % 2, :],
                                        ALU.subtract).then_inc(q_lo, 1)

            for half in range(2):
                for i in range(HB):
                    n = half * HB + i
                    dve.wait_ge(xT_done, n + 1)
                    if half and i == 0:
                        dve.wait_ge(qp_done, PAIRS)
                    nc.vector.tensor_copy(xnT[:, :, i * T:(i + 1) * T], ps_t[:, n % 2, :, :]).then_inc(xT_copied, 1)
                for p in range(PAIRS):
                    q_low(half * PAIRS + p)

            with dve.Fori(0, B) as b:
                for g in range(NQ):
                    keys = slice(g * QT, (g + 1) * QT)
                    for p in range(PAIRS):
                        dve.wait_ge(k_hi, b * (NQ * PAIRS) + (PAIRS * g + p + 1))
                        nc.vector.tensor_tensor(kT[XD:P, 0, p, keys], ps_s[0:XD, p, :], kT[0:XD, 0, p, keys],
                                                ALU.subtract)
                        nc.vector.tensor_tensor(kT[0:XD, 1, p, keys], ps_s[XD:P, p, :], kT[XD:P, 1, p, keys],
                                                ALU.subtract).then_inc(k_lo, 1)

                def maxes(h):
                    for j in range(2):
                        dve.wait_ge(s_done, AHEAD + b * (2 * XH) + (2 * h + j + 1))
                        nc.vector.tensor_reduce(smax[:, h, j:j + 1], ps_s[:, 2 * j:2 * j + 2, :]
                                                .rearrange("p a n -> p (a n)"), AX_X, ALU.max).then_inc(max_done, 1)
                    dve.wait_ge(max_done, b * (2 * XH) + 2 * (h + 1))
                    nc.vector.tensor_scalar(nmax[:, h:h + 1], smax[:, h, 0:1], smax[:, h, 1:2], -X_SCALE,
                                            ALU.max, ALU.mult).then_inc(nmax_done, 1)

                def copy_even(p):
                    for j in range(4):
                        dve.wait_ge(t_done, b * (4 * XH) + (4 * (2 * p) + j + 1))
                        nc.vector.tensor_copy(pT[:, 0, 4 * j:4 * j + 4, :], ps_t[:, j % 2, :, :]).then_inc(pT_even, 1)

                for p in range(PAIRS):
                    maxes(2 * p)
                    maxes(2 * p + 1)
                    copy_even(p)
                dve.wait_ge(exp_done, AHEAD + (b + 1) * (2 * XH))
                nc.vector.tensor_tensor(rtot[:, :], rsum[:, :, 0], rsum[:, :, 1], ALU.add).then_inc(sum_done, 1)
                dve.wait_ge(sum_done, 2 * b + 1)
                nc.vector.reciprocal(rinv[:, :], rtot[:, :]).then_inc(sum_done, 1)
                dve.wait_ge(sum_done, 2 * b + 2)
                nc.vector.tensor_copy(spread[:, :, :], rinv[:, :].unsqueeze(2).broadcast_to([P, XH, XD])) \
                    .then_inc(spread_done, 1)
                dve.wait_ge(o_stored, AHEAD + b * 16)
                dve.wait_ge(r_done, b + 1)
                nc.vector.tensor_copy(on[:, :, :], ps_r[:, :, :]).then_inc(r_copied, 1)
                dve.wait_ge(r_copied, b + 1)
                nc.vector.tensor_tensor(on[:, :, :], ps_o[:, :, :], on[:, :, :], ALU.mult).then_inc(on_done, 1)


def self_attention(nc, x_ap, bo_ap, wxo_ap, wq_ap, wkd_ap, wvd_ap, wku_ap, wvu_ap, wo_ap, wg_ap, up_ap, down_ap,
                   o_dram, rows_dram, x2, xn3, logits, wu, wd, w_loaded):
    with ExitStack() as ctx:
        def sb(name, shape, dt=F32):
            return ctx.enter_context(nc.sbuf_tensor(name, shape, dt))

        def sem(name):
            return ctx.enter_context(nc.semaphore(name))

        NI = B // 2
        DC2 = SH * SD // P
        wxo = sb("wxo", [P, PAIRS, D])
        wq = sb("wq2", [P, DC, SH * SD])
        wdown = sb("wdown", [P, DC, 4 * LAT])
        wup = sb("wup", [P, 4, SD])
        wo = sb("wo2", [P, DC2, D])
        wg = sb("wg", [P, DC, E])
        bo = sb("bo", [P, D])
        ident = sb("ident2", [P, P])
        mask = sb("mask", [P, P])
        mhalf = sb("mhalf2", [P, 1])
        hold = sb("hold", [P, 2, 2, 1])
        o_in = sb("o_in", [P, 2, PAIRS, P])
        x1 = sb("x1", [P, 2, D])
        xn = sb("xn", [P, 2, D])
        xnT = sb("xnT", [P, 2, DC, T])
        qT = sb("qT", [P, 2, SH, T])
        lat = sb("lat", [P, 2, T])
        kT = sb("kT2", [P, 2, SKV, T])
        v = sb("v2", [P, 2, SKV, SD])
        sm = sb("sm", [P, 2, SKV, REP, T])
        pT = sb("pT2", [P, 2, SKV, REP, T])
        yT = sb("yT", [P, 2, SH, T])
        x3T = sb("x3T", [P, 2, DC, T])
        stats = sb("stats2", [P, 2, 2, 6])
        mv = sb("mv2", [P, 2, 2, 2])
        rstd = sb("rstd2", [P, 2, 2, 1])
        mx = sb("mx2", [P, 2, SKV, REP])
        sums = sb("sums2", [P, 2, SKV, REP])
        inv = sb("inv2", [P, 2, SKV, REP])

        banks = [ctx.enter_context(nc.psum_tensor(f"bank{i}", [P, 512], F32)) for i in range(8)]

        ORDER = ("out0 out1 xT0 qa0 qb0 lat0 xT1 kT0 v0 sc00 sc01 qa1 qb1 lat1 kT1 v1 sc10 sc11 "
                 "pT00 pT01 y00 y01 wo0 pT10 pT11 y10 y11 x3T0 wo1 lg0 x3T1 lg1").split()
        NB = 8
        USES = len(ORDER) // NB
        assert USES * NB == len(ORDER)
        filled = [sem(f"filled{i}") for i in range(NB)]
        copied = [sem(f"copied{i}") for i in range(NB)]

        def where(name):
            return ORDER.index(name) % NB, ORDER.index(name) // NB

        def bank(name):
            return banks[where(name)[0]][:, :]

        def await_filled(eng, it, name):
            i, n = where(name)
            eng.wait_ge(filled[i], it * USES + (n + 1))

        def await_copied(eng, it, name):
            i, n = where(name)
            eng.wait_ge(copied[i], it * USES + (AHEAD + n + 1))

        def await_empty(eng, it, name):
            i, n = where(name)
            eng.wait_ge(copied[i], it * USES + (AHEAD + n))

        bo_in = sem("bo_in")
        wxo_in = sem("wxo_in")
        wq_in = sem("wq_in2")
        wkv_in = sem("wkv_in")
        wo_in = sem("wo_in")
        wup_zero = sem("wup_zero")
        consts = sem("consts")
        o_got = [sem("o_got0"), sem("o_got1")]
        x_got = [sem("x_got0"), sem("x_got1")]
        xb_done = sem("xb_done")
        dve_step = sem("dve_step")
        var_done = sem("var_done")
        rstd_done = sem("rstd_done2")
        xn_done = sem("xn_done2")
        sub_done = sem("sub_done")
        exp_done = sem("exp_done2")
        p_done = sem("p_done")
        x2_done = sem("x2_done")
        kept = sem("kept")
        xn3_stored = sem("xn3_stored")

        block = ctx.enter_context(nc.Block())

        @block.sync
        def _(sp):
            sp.dma_start(wxo[:, :, :], wxo_ap.rearrange("(c p) n -> p c n", p=P)).then_inc(wxo_in, 16)
            sp.dma_start(bo[:, :], bo_ap.rearrange("(a n) -> a n", a=1).broadcast_to([P, D])).then_inc(bo_in, 16)
            sp.dma_start(wq[:, :, :], wq_ap.rearrange("(c p) n -> p c n", p=P)).then_inc(wq_in, 16)
            for i, ap in enumerate((wkd_ap, wvd_ap)):
                sp.dma_start(wdown[:, :, 2 * LAT * i:2 * LAT * (i + 1)], ap.rearrange("(c p) n -> p c n", p=P)) \
                    .then_inc(wkv_in, 16)
            sp.wait_ge(wup_zero, 1)
            for i in range(4):
                sp.dma_start(wup[LAT * i:LAT * (i + 1), i, :], (wku_ap, wvu_ap)[i // 2]).then_inc(wkv_in, 16)
            for w, ap in ((wo, wo_ap), (wg, wg_ap)):
                sp.dma_start(w[:, :, :], ap.rearrange("(c p) n -> p c n", p=P)).then_inc(wo_in, 16)
            for s in range(2):
                sp.dma_start(wu[:, s], up_ap[s].rearrange("(c p) n -> p c n", p=P)).then_inc(w_loaded[s], 16)
                sp.dma_start(wd[:, s], down_ap[s].rearrange("(c p) n -> p c n", p=P)).then_inc(w_loaded[s], 16)
            sp.wait_ge(kept, AHEAD + 2 * B)
            sp.dma_start(rows_dram[0:B].rearrange("s t d -> t s d"), xn3[:, :, :]).then_inc(xn3_stored, 16)
            sp.wait_ge(xn3_stored, 16)
            for s in range(2):
                sp.wait_ge(w_loaded[s], 32)

        @block.gpsimd
        def _(pool):
            for count in (xn_done, kept, *copied):
                pool.sem_inc(count, AHEAD)
            pool.memset(wup[:, :, :], 0.0).then_inc(wup_zero, 1)
            pool.memset(mhalf[:, :], -0.5).then_inc(consts, 1)
            pool.memset(ident[:, :], 0.0).then_inc(consts, 1)
            pool.memset(mask[:, :], 0.0).then_inc(consts, 1)
            pool.wait_ge(consts, 3)
            pool.affine_select(out=ident[:, :], in_=ident[:, :], compare_op=ALU.not_equal, fill=1.0, base=0,
                               pattern=[[-1, P]], channel_multiplier=1).then_inc(consts, 1)
            pool.affine_select(out=mask[:, :], in_=mask[:, :], compare_op=ALU.is_ge, fill=-3.0e38, base=0,
                               pattern=[[-1, P]], channel_multiplier=1).then_inc(consts, 1)
            pool.wait_ge(consts, 5)
            pool.wait_ge(bo_in, 16)

            def rsqrt(it, k, s):
                pool.wait_ge(var_done, it * 4 + (2 * k + s + 1))
                nc.gpsimd.tensor_tensor(rstd[:, k, s, :], rstd[:, k, s, :], mhalf[:, :], ALU.pow) \
                    .then_inc(rstd_done, 1)

            with pool.Fori(0, NI) as it:
                for s in range(2):
                    pool.wait_ge(x_got[s], it * 16 + 16)
                    nc.gpsimd.tensor_tensor(x1[:, s, :], x1[:, s, :], bo[:, :], ALU.add).then_inc(xb_done, 1)
                for s in range(2):
                    rsqrt(it, 0, s)
                for s in range(2):
                    rsqrt(it, 1, s)
                    seq = bass.ds(it * 2 + s, 1)
                    nc.gpsimd.tensor_copy(x2[:, seq, :].rearrange("p o d -> p (o d)"), x1[:, s, :]) \
                        .then_inc(kept, 1)
                    pool.wait_ge(xn_done, it * 4 + (AHEAD + 2 + s + 1))
                    nc.gpsimd.tensor_copy(xn3[:, seq, :].rearrange("p o d -> p (o d)"), xn[:, s, :]) \
                        .then_inc(kept, 1)

        @block.tensor
        def _(pe):
            def accumulate(out, pieces):
                for c, (w, m) in enumerate(pieces):
                    mm = nc.tensor.matmul(out, w, m, start=(c == 0), stop=(c == len(pieces) - 1))
                return mm

            def fill(mm, name):
                mm.then_inc(filled[where(name)[0]], 1)

            def transpose_all(name, tiles):
                for c, tile in enumerate(tiles):
                    mm = nc.tensor.transpose(bank(name)[:, c * P:(c + 1) * P], tile, ident[:, :])
                fill(mm, name)

            pe.wait_ge(consts, 5)
            pe.wait_ge(wxo_in, 16)
            with pe.Fori(0, NI) as it:
                def project_cross(s):
                    name = f"out{s}"
                    await_empty(pe, it, name)
                    pe.wait_ge(o_got[s], it * 16 + 16)
                    fill(accumulate(bank(name), [(o_in[:, s, p, :], wxo[:, p, :]) for p in range(PAIRS)]), name)

                def turn_norm(k, s):
                    name = ("xT", "x3T")[k] + str(s)
                    await_empty(pe, it, name)
                    pe.wait_ge(xn_done, it * 4 + (AHEAD + 2 * k + s + 1))
                    transpose_all(name, [xn[:, s, c * P:(c + 1) * P] for c in range(DC)])

                def queries(s):
                    await_copied(pe, it, f"xT{s}")
                    for n in range(2):
                        name = f"q{'ab'[n]}{s}"
                        await_empty(pe, it, name)
                        for i in range(4):
                            h = 4 * n + i
                            mm = accumulate(bank(name)[:, i * T:(i + 1) * T],
                                            [(wq[:, c, h * SD:(h + 1) * SD], xnT[:, s, c, :]) for c in range(DC)])
                        fill(mm, name)

                def latents(s):
                    await_empty(pe, it, f"lat{s}")
                    fill(accumulate(bank(f"lat{s}")[:, 0:T], [(wdown[:, c, :], xnT[:, s, c, :]) for c in range(DC)]),
                         f"lat{s}")

                def keys_values(s):
                    await_copied(pe, it, f"lat{s}")
                    await_empty(pe, it, f"kT{s}")
                    for g in range(SKV):
                        mm = accumulate(bank(f"kT{s}")[:, g * T:(g + 1) * T], [(wup[:, g, :], lat[:, s, :])])
                    fill(mm, f"kT{s}")
                    await_empty(pe, it, f"v{s}")
                    fill(accumulate(bank(f"v{s}")[:, 0:SKV * SD], [(lat[:, s, :], wup[:, 2:4, :])]), f"v{s}")

                def scores(s):
                    for name in (f"qa{s}", f"qb{s}", f"kT{s}"):
                        await_copied(pe, it, name)
                    for g in range(SKV):
                        name = f"sc{s}{g}"
                        await_empty(pe, it, name)
                        for r in range(REP):
                            mm = accumulate(bank(name)[:, r * T:(r + 1) * T],
                                            [(qT[:, s, g * REP + r, :], kT[:, s, g, :])])
                        fill(mm, name)

                def turn_probs(s):
                    for g in range(SKV):
                        name = f"pT{s}{g}"
                        await_empty(pe, it, name)
                        pe.wait_ge(p_done, it * 4 + (2 * s + g + 1))
                        transpose_all(name, [sm[:, s, g, r, :] for r in range(REP)])

                def values(s):
                    await_copied(pe, it, f"v{s}")
                    for g in range(SKV):
                        name = f"y{s}{g}"
                        await_empty(pe, it, name)
                        await_copied(pe, it, f"pT{s}{g}")
                        fill(accumulate(bank(name), [(v[:, s, g, :], pT[:, s, g, :, :])]), name)

                def project(s):
                    name = f"wo{s}"
                    await_empty(pe, it, name)
                    for g in range(SKV):
                        await_copied(pe, it, f"y{s}{g}")
                    fill(accumulate(bank(name), [(yT[:, s, h, :], wo[:, h, :]) for h in range(SH)]), name)

                def route(s):
                    name = f"lg{s}"
                    await_empty(pe, it, name)
                    await_copied(pe, it, f"x3T{s}")
                    fill(accumulate(bank(name)[:, 0:E], [(x3T[:, s, c, :], wg[:, c, :]) for c in range(DC)]), name)

                project_cross(0)
                project_cross(1)
                turn_norm(0, 0)
                pe.wait_ge(wq_in, 16)
                queries(0)
                pe.wait_ge(wkv_in, 16 * 6)
                latents(0)
                turn_norm(0, 1)
                keys_values(0)
                scores(0)
                queries(1)
                latents(1)
                keys_values(1)
                scores(1)
                turn_probs(0)
                values(0)
                pe.wait_ge(wo_in, 32)
                project(0)
                turn_probs(1)
                values(1)
                turn_norm(1, 0)
                project(1)
                route(0)
                turn_norm(1, 1)
                route(1)

        def evacuate(eng, it, name, dst, src, copy):
            await_filled(eng, it, name)
            copy(dst, src).then_inc(copied[where(name)[0]], 1)

        @block.scalar
        def _(act):
            def copy(dst, src):
                return nc.scalar.activation(dst, src, ACT.Copy)

            with act.Fori(0, NI) as it:
                def take(name, dst):
                    n = 1
                    for k in dst.shape[1:]:
                        n *= k
                    src = bank(name)[:, 0:n]
                    if len(dst.shape) == 3:
                        src = src.rearrange("p (a t) -> p a t", a=dst.shape[1])
                    evacuate(act, it, name, dst, src, copy)

                def exps(s):
                    for g in range(SKV):
                        act.wait_ge(sub_done, it * 4 + (2 * s + g + 1))
                        t = sm[:, s, g]
                        nc.scalar.activation(t, t, ACT.Exp).then_inc(exp_done, 1)

                for s in range(2):
                    await_empty(act, it, "lat0")
                    act.wait_ge(xn_done, it * 4 + AHEAD)
                    act.wait_ge(kept, it * 4 + AHEAD)
                    act.dma_start(o_in[:, s], o_dram[bass.ds(it * 2 + s, 1)].rearrange("o p h t -> (o p) h t")) \
                        .then_inc(o_got[s], 16)
                    act.dma_start(x1[:, s], x_ap[bass.ds(it * 2 + s, 1)].rearrange("o t d -> (o t) d")) \
                        .then_inc(x_got[s], 16)
                take("xT0", xnT[:, 0])
                take("qa0", qT[:, 0, 0:4])
                take("lat0", lat[:, 0])
                take("xT1", xnT[:, 1])
                take("v0", v[:, 0])
                exps(0)
                take("qa1", qT[:, 1, 0:4])
                take("lat1", lat[:, 1])
                take("v1", v[:, 1])
                take("pT00", pT[:, 0, 0])
                take("pT01", pT[:, 0, 1])
                exps(1)
                take("y00", yT[:, 0, 0:REP])
                take("pT10", pT[:, 1, 0])
                take("pT11", pT[:, 1, 1])
                take("y10", yT[:, 1, 0:REP])
                take("x3T0", x3T[:, 0])
                take("x3T1", x3T[:, 1])

        @block.vector
        def _(dve):
            STEPS = 2 * 4 + 4 + 2 * 4

            with dve.Fori(0, NI) as it:
                steps = [0]

                def link(ins):
                    steps[0] += 1
                    ins.then_inc(dve_step, 1)
                    dve.wait_ge(dve_step, it * STEPS + steps[0])

                def take(name, dst):
                    src = bank(name)[:, 0:dst.shape[1] * dst.shape[2]].rearrange("p (a t) -> p a t", a=dst.shape[1])
                    evacuate(dve, it, name, dst, src, nc.vector.tensor_copy)

                def add(name, k, s):
                    await_filled(dve, it, name)
                    nc.vector.tensor_tensor(x1[:, s, :], bank(name), x1[:, s, :], ALU.add) \
                        .then_inc(copied[where(name)[0]], 1)
                    await_copied(dve, it, name)
                    link(nc.vector.bn_stats(stats[:, k, s, :], x1[:, s, :]))
                    nc.vector.memset(hold[:, k, s, :], 0.0)
                    link(nc.vector.bn_aggr(mv[:, k, s, :], stats[:, k, s, :]))
                    nc.vector.tensor_scalar(rstd[:, k, s, :], mv[:, k, s, 1:2], EPS, None, ALU.add) \
                        .then_inc(var_done, 1)

                def norm(k, s):
                    dve.wait_ge(rstd_done, it * 4 + (2 * k + s + 1))
                    nc.vector.tensor_scalar(xn[:, s, :], x1[:, s, :], mv[:, k, s, 0:1], rstd[:, k, s, :],
                                            ALU.subtract, ALU.mult).then_inc(xn_done, 1)

                def shift(s):
                    for g in range(SKV):
                        name = f"sc{s}{g}"
                        await_filled(dve, it, name)
                        t = sm[:, s, g]
                        nc.vector.scalar_tensor_tensor(
                            out=t, in0=bank(name).rearrange("p (r t) -> p r t", r=REP), scalar=S_SCALE,
                            in1=mask[:, :].unsqueeze(1).broadcast_to([P, REP, T]), op0=ALU.mult, op1=ALU.add) \
                            .then_inc(copied[where(name)[0]], 1)
                        await_copied(dve, it, name)
                        link(nc.vector.tensor_reduce(mx[:, s, g, :], t, AX_X, ALU.max))
                        nc.vector.tensor_tensor(t, t, mx[:, s, g, :].unsqueeze(2).broadcast_to([P, REP, T]),
                                                ALU.subtract).then_inc(sub_done, 1)

                def normalise(s):
                    for g in range(SKV):
                        dve.wait_ge(exp_done, it * 4 + (2 * s + g + 1))
                        t = sm[:, s, g]
                        link(nc.vector.tensor_reduce(sums[:, s, g, :], t, AX_X, ALU.add))
                        link(nc.vector.reciprocal(inv[:, s, g, :], sums[:, s, g, :]))
                        nc.vector.tensor_tensor(t, t, inv[:, s, g, :].unsqueeze(2).broadcast_to([P, REP, T]),
                                                ALU.mult).then_inc(p_done, 1)

                for s in range(2):
                    dve.wait_ge(xb_done, it * 2 + (s + 1))
                    add(f"out{s}", 0, s)
                for s in range(2):
                    norm(0, s)
                take("qb0", qT[:, 0, 4:8])
                take("kT0", kT[:, 0])
                shift(0)
                take("qb1", qT[:, 1, 4:8])
                normalise(0)
                take("kT1", kT[:, 1])
                shift(1)
                take("y01", yT[:, 0, REP:SH])
                normalise(1)
                add("wo0", 1, 0)
                take("y11", yT[:, 1, REP:SH])
                norm(1, 0)
                add("wo1", 1, 1)
                for s in range(2):
                    if s:
                        norm(1, 1)
                    evacuate(dve, it, f"lg{s}", logits[:, bass.ds(it * 2 + s, 1), :].rearrange("p o e -> p (o e)"),
                             bank(f"lg{s}")[:, 0:E], nc.vector.tensor_copy)
                assert steps[0] == STEPS, steps


def experts(nc, up_ap, down_ap, out_ap, rows_dram, x2, xn3, logits, wu, wd, w_loaded):
    with ExitStack() as ctx:
        def sb(name, shape, dt=F32):
            return ctx.enter_context(nc.sbuf_tensor(name, shape, dt))

        def sem(name):
            return ctx.enter_context(nc.semaphore(name))

        FC = F // P
        NT = B * T // P
        ident = sb("ident3", [P, P])
        before = sb("before", [P, P])
        ones = sb("ones3", [P, P])
        row = sb("row", [P, D])
        rowT = sb("rowT", [P, DC, P])
        gT = sb("gT", [P, FC, P])
        y = sb("y", [P, D])
        picked = sb("picked", [P, 2, NT, D])
        hold = sb("hold3", [P, 1])
        iota = sb("iota", [P, E])
        thr = sb("thr", [P, NT - 1])
        probs = sb("probs3", [P, NT, E])
        lmax = sb("lmax", [P, NT])
        den = sb("den", [P, NT])
        rden = sb("rden3", [P, NT])
        top = sb("top", [P, NT, 8])
        index = sb("index", [P, NT, 8], U32)
        index_f = sb("index_f", [P, NT, 2])
        weight = sb("weight", [P, NT, 2])
        hit = sb("hit", [P, 2, NT, E])
        both = sb("both", [P, NT, E])
        rank = sb("rank", [P, NT, E])
        earlier = sb("earlier", [P, NT + 1, E])
        full = sb("full", [P, E, NT - 1])
        n_tiles = sb("n_tiles", [P, E])
        first = sb("first", [P, E + 1])
        first_i = sb("first_i", [P, E + 1], U32)
        slot = sb("slot", [P, 2, NT])
        slot_i = sb("slot_i", [P, 2, NT], U32)

        up_ps = ctx.enter_context(nc.psum_tensor("up_ps", [P, 2, 4, P], F32))
        down_ps = ctx.enter_context(nc.psum_tensor("down_ps", [P, D], F32))
        rowT_ps = ctx.enter_context(nc.psum_tensor("rowT_ps", [P, DC, P], F32))
        rank_ps = ctx.enter_context(nc.psum_tensor("rank_ps", [P, NT, E], F32, ))
        total_ps = ctx.enter_context(nc.psum_tensor("total_ps", [P, 512], F32))

        consts = sem("consts3")
        route = sem("route")
        e_done = sem("e_done")
        hits_done = sem("hits_done")
        counted = sem("counted")
        slots_done = sem("slots_done")
        firsts_done = sem("firsts_done")
        rows_sent = sem("rows_sent")
        row_in = sem("row_in")
        rowT_done = sem("rowT_done")
        rowT_copied = sem("rowT_copied")
        up_done = sem("up_done")
        gelu_done = sem("gelu_done")
        down_done = sem("down_done")
        y_copied = sem("y_copied")
        y_stored = sem("y_stored")
        got = [sem(f"got{t}") for t in range(NT)]
        mixed = sem("mixed")
        out_stored = sem("out_stored")

        block = ctx.enter_context(nc.Block())

        def bounds(eng, e):
            lo = eng.value_load(first_i[0:1, bass.ds(e, 1)], min_val=NT, max_val=MAX_TILES)
            hi = eng.value_load(first_i[0:1, bass.ds(e + 1, 1)], min_val=NT + 1, max_val=MAX_TILES)
            return lo, hi

        @block.sync
        def _(sp):
            def load_weights(s, par, done):
                sp.wait_ge(down_done, done)
                sp.dma_start(wu[:, par], up_ap[bass.ds(s, 1)].rearrange("o (c p) n -> p (o c) n", p=P)) \
                    .then_inc(w_loaded[par], 16)
                sp.dma_start(wd[:, par], down_ap[bass.ds(s, 1)].rearrange("o (c p) n -> p (o c) n", p=P)) \
                    .then_inc(w_loaded[par], 16)

            def store_tiles(e):
                with sp.Fori(*bounds(sp, e)) as t:
                    sp.wait_ge(y_copied, t + (AHEAD + 1))
                    sp.dma_start(rows_dram[bass.ds(t, 1)].rearrange("o p d -> (o p) d"), y[:, :]).then_inc(y_stored, 16)

            sp.wait_ge(firsts_done, 1)
            with sp.Fori(0, E // 2 - 1) as j:
                for k in range(2):
                    done = sp.value_load(first_i[0:1, bass.ds(j * 2 + k, 1)], min_val=NT, max_val=MAX_TILES)
                    load_weights(j * 2 + (k + 2), k, done)
                    store_tiles(j * 2 + k)
            done = sp.value_load(first_i[0:1, E - 2:E - 1], min_val=NT, max_val=MAX_TILES)
            load_weights(E, 0, done)
            for e in (E - 2, E - 1):
                store_tiles(e)
            for t in range(NT):
                sp.wait_ge(mixed, 2 * (t + 1))
                sp.dma_start(out_ap[t], x2[:, t, :]).then_inc(out_stored, 16)
            sp.wait_ge(out_stored, 16 * NT)

        @block.gpsimd
        def _(pool):
            pool.sem_inc(y_stored, 16 * NT)
            pool.memset(ident[:, :], 0.0).then_inc(consts, 1)
            pool.memset(before[:, :], 0.0).then_inc(consts, 1)
            pool.memset(ones[:, :], 1.0).then_inc(consts, 1)
            pool.memset(hold[:, :], 0.0).then_inc(consts, 1)
            pool.iota(iota[:, :], pattern=[[1, E]], base=0, channel_multiplier=0,
                      allow_small_or_imprecise_dtypes=True).then_inc(consts, 1)
            pool.iota(thr[:, :], pattern=[[P, NT - 1]], base=P, channel_multiplier=0,
                      allow_small_or_imprecise_dtypes=True).then_inc(consts, 1)
            pool.wait_ge(consts, 6)
            pool.affine_select(out=ident[:, :], in_=ident[:, :], compare_op=ALU.not_equal, fill=1.0, base=0,
                               pattern=[[-1, P]], channel_multiplier=1).then_inc(consts, 1)
            pool.affine_select(out=before[:, :], in_=before[:, :], compare_op=ALU.is_ge, fill=1.0, base=0,
                               pattern=[[-1, P]], channel_multiplier=1).then_inc(consts, 1)
            pool.wait_ge(slots_done, 1)
            for t in range(NT):
                for k in range(2):
                    pool.indirect_dma_start(
                        out=rows_dram.rearrange("n p d -> (n p) d"),
                        out_offset=bass.IndirectOffsetOnAxis(ap=slot_i[:, k, t:t + 1], axis=0),
                        in_=xn3[:, t, :], in_offset=None).then_inc(rows_sent, 16)
            pool.wait_ge(firsts_done, 1)
            pool.wait_ge(rows_sent, 16 * 2 * NT)
            end = pool.value_load(first_i[0:1, E:E + 1], min_val=NT, max_val=MAX_TILES)
            pool.wait_ge(y_stored, end * 16)
            nc.gpsimd.tensor_tensor(hold[:, :], hold[:, :], hold[:, :], ALU.add)
            for t in range(NT):
                for k in range(2):
                    pool.indirect_dma_start(
                        out=picked[:, k, t, :], out_offset=None,
                        in_=rows_dram.rearrange("n p d -> (n p) d"),
                        in_offset=bass.IndirectOffsetOnAxis(ap=slot_i[:, k, t:t + 1], axis=0)).then_inc(got[t], 16)

        @block.tensor
        def _(pe):
            def turn(n):
                pe.wait_ge(row_in, n * 16 + 16)
                pe.wait_ge(rowT_copied, n + AHEAD)
                for c in range(DC):
                    mm = nc.tensor.transpose(rowT_ps[:, c, :], row[:, c * P:(c + 1) * P], ident[:, :])
                mm.then_inc(rowT_done, 1)

            def tile(t, par):
                pe.wait_ge(rowT_copied, t + (AHEAD + 1))
                for n in range(2):
                    pe.wait_ge(gelu_done, t * 2 + (n + 1 - 2 + 2 * AHEAD))
                    for i in range(4):
                        f = 4 * n + i
                        for c in range(DC):
                            mm = nc.tensor.matmul(up_ps[:, n, i, :], wu[:, par, c, f * P:(f + 1) * P], rowT[:, c, :],
                                                  start=(c == 0), stop=(c == DC - 1))
                    mm.then_inc(up_done, 1)
                turn(t + 1)
                pe.wait_ge(y_copied, t + AHEAD)
                for f in range(FC):
                    if f % 4 == 0:
                        pe.wait_ge(gelu_done, t * 2 + (f // 4 + 1 + AHEAD))
                    mm = nc.tensor.matmul(down_ps[:, :], gT[:, f, :], wd[:, par, f, :],
                                          start=(f == 0), stop=(f == FC - 1))
                mm.then_inc(down_done, 1)

            pe.wait_ge(consts, 8)
            turn(0)
            tile(0, 0)
            pe.wait_ge(hits_done, 1)
            nc.tensor.matmul(rank_ps[:, :, :], before[:, :], both[:, :, :], start=True, stop=True)
            nc.tensor.matmul(total_ps[:, 0:NT * E], ones[:, :], both[:, :, :], start=True, stop=True) \
                .then_inc(counted, 1)
            with pe.Fori(1, NT) as t:
                tile(t, 0)
            pe.wait_ge(firsts_done, 1)
            with pe.Fori(0, E // 2) as j:
                for k in range(2):
                    with pe.Fori(*bounds(pe, j * 2 + k)) as t:
                        pe.wait_ge(w_loaded[1 - k], j * 32 + (32 + 32 * k))
                        tile(t, 1 - k)

        @block.scalar
        def _(act):
            def load_row(n):
                act.dma_start(row[:, :], rows_dram[bass.ds(n, 1)].rearrange("o p d -> (o p) d")).then_inc(row_in, 16)

            def tile(t, before_load=None):
                act.wait_ge(rowT_done, t + 1)
                if before_load:
                    before_load()
                load_row(t + 1)
                for n in range(2):
                    act.wait_ge(up_done, t * 2 + (n + 1))
                    nc.scalar.activation(gT[:, 4 * n:4 * n + 4, :], up_ps[:, n], ACT.Gelu).then_inc(gelu_done, 1)

            act.sem_inc(gelu_done, AHEAD)
            act.dma_start(row[:, :], rows_dram[0]).then_inc(row_in, 16)
            act.wait_ge(route, 2)
            nc.scalar.activation(probs[:, :, :], probs[:, :, :], ACT.Exp).then_inc(e_done, 1)
            with act.Fori(0, NT - 1) as t:
                tile(t)
            tile(NT - 1, lambda: act.wait_ge(rows_sent, 16 * 2 * NT))
            act.wait_ge(firsts_done, 1)
            with act.Fori(0, E) as e:
                with act.Fori(*bounds(act, e)) as t:
                    tile(t)
            act.wait_ge(row_in, 16)

        @block.vector
        def _(dve):
            steps = [0]

            def link(ins):
                steps[0] += 1
                ins.then_inc(route, 1)
                dve.wait_ge(route, steps[0])

            def copy_rowT(n):
                dve.wait_ge(rowT_done, n + 1)
                nc.vector.tensor_copy(rowT[:, :, :], rowT_ps[:, :, :]).then_inc(rowT_copied, 1)

            def add_shared(t):
                dve.wait_ge(down_done, t + 1)
                x2t = x2[:, bass.ds(t, 1), :].rearrange("p o d -> p (o d)")
                nc.vector.tensor_tensor(x2t, down_ps[:, :], x2t, ALU.add).then_inc(y_copied, 1)

            def spread(ap):
                return ap.unsqueeze(2).broadcast_to([P, NT, E])

            dve.sem_inc(rowT_copied, AHEAD)
            dve.sem_inc(y_copied, AHEAD)
            copy_rowT(0)
            link(nc.vector.tensor_reduce(lmax[:, :], logits[:, :, :], AX_X, ALU.max))
            link(nc.vector.tensor_tensor(probs[:, :, :], logits[:, :, :], spread(lmax[:, :]), ALU.subtract))
            dve.wait_ge(e_done, 1)
            link(nc.vector.tensor_reduce(den[:, :], probs[:, :, :], AX_X, ALU.add))
            link(nc.vector.reciprocal(rden[:, :], den[:, :]))
            link(nc.vector.tensor_tensor(probs[:, :, :], probs[:, :, :], spread(rden[:, :]), ALU.mult))
            for t in range(NT):
                last = nc.vector.max(top[:, t, :], probs[:, t, :])
            link(last)
            for t in range(NT):
                last = nc.vector.max_index(index[:, t, :], top[:, t, :], probs[:, t, :])
            link(last)
            link(nc.vector.tensor_copy(index_f[:, :, :], index[:, :, 0:2]))
            dve.wait_ge(consts, 8)
            for k in range(2):
                link(nc.vector.tensor_tensor(hit[:, k], iota[:, :].unsqueeze(1).broadcast_to([P, NT, E]),
                                             index_f[:, :, k:k + 1].broadcast_to([P, NT, E]), ALU.is_equal))
            nc.vector.tensor_tensor(both[:, :, :], hit[:, 0], hit[:, 1], ALU.add).then_inc(hits_done, 1)
            link(nc.vector.tensor_tensor(den[:, :], top[:, :, 0], top[:, :, 1], ALU.add))
            link(nc.vector.reciprocal(rden[:, :], den[:, :]))
            link(nc.vector.tensor_tensor(weight[:, :, :], top[:, :, 0:2], rden[:, :].unsqueeze(2)
                                         .broadcast_to([P, NT, 2]), ALU.mult))
            link(nc.vector.memset(earlier[:, 0, :], 0.0))
            link(nc.vector.memset(first[:, 0:1], float(NT)))
            copy_rowT(1)
            add_shared(0)
            dve.wait_ge(counted, 1)
            for t in range(NT):
                link(nc.vector.tensor_tensor(earlier[:, t + 1, :], total_ps[:, t * E:(t + 1) * E], earlier[:, t, :],
                                             ALU.add))
            link(nc.vector.tensor_tensor(full[:, :, :], earlier[:, NT, :].unsqueeze(2).broadcast_to([P, E, NT - 1]),
                                         thr[:, :].unsqueeze(1).broadcast_to([P, E, NT - 1]), ALU.is_gt))
            link(nc.vector.tensor_reduce(n_tiles[:, :], full[:, :, :], AX_X, ALU.add))
            for e in range(E):
                link(nc.vector.tensor_scalar(first[:, e + 1:e + 2], n_tiles[:, e:e + 1], first[:, e:e + 1], 1.0,
                                             ALU.add, ALU.add))
            nc.vector.tensor_copy(first_i[:, :], first[:, :]).then_inc(firsts_done, 1)
            link(nc.vector.tensor_tensor(rank[:, :, :], rank_ps[:, :, :], earlier[:, 0:NT, :], ALU.add))
            link(nc.vector.scalar_tensor_tensor(out=rank[:, :, :], in0=first[:, 0:E].unsqueeze(1)
                                                .broadcast_to([P, NT, E]), scalar=float(P), in1=rank[:, :, :],
                                                op0=ALU.mult, op1=ALU.add))
            for k in range(2):
                link(nc.vector.tensor_tensor(hit[:, k], hit[:, k], rank[:, :, :], ALU.mult))
                link(nc.vector.tensor_reduce(slot[:, k, :], hit[:, k], AX_X, ALU.add))
            nc.vector.tensor_copy(slot_i[:, :, :], slot[:, :, :]).then_inc(slots_done, 1)
            with dve.Fori(1, NT) as t:
                copy_rowT(t + 1)
                add_shared(t)
            dve.wait_ge(firsts_done, 1)
            with dve.Fori(0, E) as e:
                with dve.Fori(*bounds(dve, e)) as t:
                    copy_rowT(t + 1)
                    dve.wait_ge(down_done, t + 1)
                    dve.wait_ge(y_stored, t * 16)
                    nc.vector.tensor_copy(y[:, :], down_ps[:, :]).then_inc(y_copied, 1)
            for t in range(NT):
                dve.wait_ge(got[t], 32)
                for k in range(2):
                    nc.vector.scalar_tensor_tensor(out=x2[:, t, :], in0=picked[:, k, t, :], scalar=weight[:, t, k:k + 1],
                                                   in1=x2[:, t, :], op0=ALU.mult, op1=ALU.add).then_inc(mixed, 1)
                    if k == 0:
                        dve.wait_ge(mixed, 2 * t + 1)


def perceiver_block(nc, x, ctx_t, xq, xk, xv, xo, xbo, sq, skd, svd, sku, svu, so, gate, up, down, out):
    q_dram = nc.dram_tensor("q_scratch", (2, PAIRS, P, B * T), F32, kind="Internal").ap()
    o_dram = nc.dram_tensor("o_scratch", (B, P, PAIRS, T), F32, kind="Internal").ap()
    rows_dram = nc.dram_tensor("rows_scratch", (MAX_TILES + 1, P, D), F32, kind="Internal").ap()
    cross_attention(nc, x, ctx_t, xq, xk, xv, q_dram, o_dram, rows_dram)
    with ExitStack() as ctx:
        x2 = ctx.enter_context(nc.sbuf_tensor("x2", [P, B, D], F32))
        xn3 = ctx.enter_context(nc.sbuf_tensor("xn3", [P, B, D], F32))
        logits = ctx.enter_context(nc.sbuf_tensor("logits", [P, B, E], F32))
        wu = ctx.enter_context(nc.sbuf_tensor("wu", [P, 2, DC, F], F32))
        wd = ctx.enter_context(nc.sbuf_tensor("wd", [P, 2, F // P, D], F32))
        w_loaded = [ctx.enter_context(nc.semaphore(f"w_loaded{i}")) for i in range(2)]
        self_attention(nc, x, xbo, xo, sq, skd, svd, sku, svu, so, gate, up, down, o_dram, rows_dram,
                       x2, xn3, logits, wu, wd, w_loaded)
        experts(nc, up, down, out, rows_dram, x2, xn3, logits, wu, wd, w_loaded)


def kernel(**inputs):
    import numpy as _np
    import concourse.bacc as _bacc
    from concourse import mybir as _mybir
    from concourse.bass_utils import run_bass_kernel_spmd as _run

    a = {k: _np.asarray(v) for k, v in inputs.items()}
    ctx_t = a["ctx_1024"].reshape(B, NQ, QT, DC, P).transpose(0, 1, 4, 3, 2)
    laid = [
        ("x", a["x"]), ("ctx", ctx_t), ("xq", a["L0_xattn_Wq"]), ("xk", a["L0_xattn_Wk"]),
        ("xv", a["L0_xattn_Wv"]), ("xo", a["L0_xattn_Wo"]), ("xbo", a["L0_xattn_bo"]),
        ("sq", a["L0_attn_wq"]), ("skd", a["L0_attn_wk_down"]), ("svd", a["L0_attn_wv_down"]),
        ("sku", a["L0_attn_wk_up"]), ("svu", a["L0_attn_wv_up"]), ("so", a["L0_attn_wo"]),
        ("gate", a["L0_ffn_Wg"]),
        ("up", _np.concatenate([a["L0_ffn_W1"][None], a["L0_ffn_Wu"]])),
        ("down", _np.concatenate([a["L0_ffn_W2"][None], a["L0_ffn_Wd"]])),
    ]
    nc = _bacc.Bacc("TRN2", target_bir_lowering=False, num_devices=1, dynamic_dma_scratch_size=4096)
    arrays, args = {}, []
    for name, v in laid:
        v = _np.ascontiguousarray(v)
        arrays[f"in_{name}_dram"] = v
        args.append(nc.dram_tensor(f"in_{name}_dram", v.shape, _mybir.dt.from_np(v.dtype), kind="ExternalInput").ap())
    args.append(nc.dram_tensor("out_0_dram", (B, T, D), _mybir.dt.float32, kind="ExternalOutput").ap())
    perceiver_block(nc, *args)
    r = _run(nc, [arrays], core_ids=[0])
    return r.results[0]["out_0_dram"]
```

```python
from contextlib import ExitStack

import concourse.bass as bass
from concourse import mybir

F32 = mybir.dt.float32
F32R = mybir.dt.float32r
U32 = mybir.dt.uint32
ALU = mybir.AluOpType
ACT = mybir.ActivationFunctionType
AX_X = mybir.AxisListType.X

P = 128
EPS = 1e-5

B, T, D = 8, 128, 512
M = 2048
XH, XD = 8, 64
SH, SKV, SD, LAT = 8, 2, 128, 32
REP = SH // SKV
E, F = 8, 1024
MAX_TILES = B * T // P + (2 * B * T - E) // P + E
DC = D // P
PAIRS = XH // 2
QT = 512
NQ = M // QT
MT = M // P
X_SCALE = XD ** -0.5
S_SCALE = SD ** -0.5

AHEAD = 1


def cross_attention(nc, x_ap, ctx_ap, wq_ap, wk_ap, wv_ap, q_dram, o_dram, rows_dram):
    with ExitStack() as ctx:
        def sb(name, shape, dt):
            return ctx.enter_context(nc.sbuf_tensor(name, shape, dt))

        def sem(name):
            return ctx.enter_context(nc.semaphore(name))

        wk = sb("wk", [P, 2, DC, D], F32R)
        wv = sb("wv", [P, 2, DC, D], F32R)
        stage = sb("stage", [P, 2, 2, QT], F32)
        ctx_h = sb("ctx_h", [P, 2, DC, QT], F32R)
        ctx_l = sb("ctx_l", [P, 2, DC, QT], F32R)
        kT = sb("kT", [P, 2, PAIRS, M], F32R)
        vt = sb("vt", [P, MT, D], F32)
        qa = sb("qa", [P, XH, T], F32R)
        qb = sb("qb", [P, XH, T], F32R)
        probs = sb("probs", [P, 2, M], F32)
        pT = sb("pT", [P, 2, MT, P], F32)
        on = sb("on", [P, PAIRS, P], F32)
        ident = sb("ident", [P, P], F32)
        one = sb("one", [P, 1], F32)
        zero = sb("zero", [P, D], F32)
        mhalf = sb("mhalf", [P, 1], F32)
        spread = sb("spread", [P, XH, XD], F32)
        smax = sb("smax", [P, XH, 2], F32)
        nmax = sb("nmax", [P, XH], F32)
        rsum = sb("rsum", [P, XH, 2], F32)
        rtot = sb("rtot", [P, XH], F32)
        rinv = sb("rinv", [P, XH], F32)
        stats = sb("stats", [P, B, 6], F32)
        mv = sb("mv", [P, B, 2], F32)
        rstd = sb("rstd", [P, B], F32)

        x_all = probs[:, :, :].rearrange("p a (b d) -> p (a b) d", d=D)
        pT_flat = pT[:, :, :, :].rearrange("p a t m -> p a (t m)")
        wq = pT_flat[:, 0, :].rearrange("p (c n) -> p c n", c=DC)
        xnT = pT_flat[:, 1, :].rearrange("p (c n) -> p c n", c=DC)
        q_halves = kT[:, :, 0:2, :].rearrange("p w h m -> p w (h m)")

        ps_s = ctx.enter_context(nc.psum_tensor("ps_s", [P, 4, 512], F32))
        ps_t = ctx.enter_context(nc.psum_tensor("ps_t", [P, 3, 4, P], F32))
        ps_o = ctx.enter_context(nc.psum_tensor("ps_o", [P, PAIRS, P], F32))
        ps_v = ps_t[:, :, :, :].rearrange("p b i m -> p b (i m)")
        ps_r = ps_t[:, 2]

        x_in = [sem("x_in0"), sem("x_in1")]
        wq_in = sem("wq_in")
        ident_ok = sem("ident_ok")
        zero_ok = sem("zero_ok")
        zeroed = sem("zeroed")
        bn_done = sem("bn_done")
        rstd_done = sem("rstd_done")
        xn_done = sem("xn_done")
        xT_done = sem("xT_done")
        xT_copied = sem("xT_copied")
        qp_done = sem("qp_done")
        q_hi = sem("q_hi")
        q_lo = sem("q_lo")
        q_stored = sem("q_stored")
        raw_in = [sem("raw_in0"), sem("raw_in1")]
        hi_done = sem("hi_done")
        split_done = sem("split_done")
        proj_done = sem("proj_done")
        k_hi = sem("k_hi")
        k_lo = sem("k_lo")
        v_copied = sem("v_copied")
        q_in = sem("q_in")
        s_done = sem("s_done")
        max_done = sem("max_done")
        nmax_done = sem("nmax_done")
        exp_done = sem("exp_done")
        t_done = sem("t_done")
        pT_even = sem("pT_even")
        pT_odd = sem("pT_odd")
        pv_done = sem("pv_done")
        sum_done = sem("sum_done")
        spread_done = sem("spread_done")
        r_done = sem("r_done")
        r_copied = sem("r_copied")
        on_done = sem("on_done")
        o_stored = sem("o_stored")

        HB = B // 2
        HT = HB * T
        NW = 2 * DC // 2
        LB = NQ * DC // 2
        GQ = PAIRS + QT // P
        GB = NQ * GQ

        block = ctx.enter_context(nc.Block())

        @block.sync
        def _(sp):
            sp.dma_start(x_all[:, 0:HB], x_ap[0:HB].rearrange("b t d -> t b d")).then_inc(x_in[0], 16)
            sp.dma_start(wq, wq_ap.rearrange("(c p) n -> p c n", p=P)).then_inc(wq_in, 16)
            for n in range(NW):
                w_ap, c = (wk_ap, wv_ap)[n // 2], 2 * (n % 2)
                if n >= 2:
                    sp.wait_ge(split_done, n - 1)
                sp.dma_start(stage[:, n % 2], w_ap[c * P:(c + 2) * P, :].rearrange("(c p) n -> p c n", p=P)) \
                    .then_inc(raw_in[n % 2], 16)
            sp.wait_ge(zero_ok, 1)
            for n in range(B * T // P, MAX_TILES + 1):
                sp.dma_start(rows_dram[n], zero[:, :]).then_inc(zeroed, 16)
            with sp.Fori(0, B) as b:
                for k in range(LB):
                    sp.wait_ge(split_done, b * LB + (NW + k - 1))
                    sp.dma_start(stage[:, k % 2],
                                 ctx_ap[bass.ds(b, 1), k // 2, :, 2 * (k % 2):2 * (k % 2) + 2, :]
                                 .rearrange("o p c m -> (o p) c m")).then_inc(raw_in[k % 2], 16)
            sp.wait_ge(zeroed, 16 * (MAX_TILES + 1 - B * T // P))

        @block.gpsimd
        def _(pool):
            for count in (s_done, exp_done, pT_even, pT_odd, r_copied, on_done, o_stored):
                pool.sem_inc(count, AHEAD)
            pool.memset(zero[:, :], 0.0).then_inc(zero_ok, 1)
            pool.memset(one[:, :], 1.0).then_inc(ident_ok, 1)
            pool.memset(mhalf[:, :], -0.5).then_inc(ident_ok, 1)
            pool.memset(ident[:, :], 0.0).then_inc(ident_ok, 1)
            pool.wait_ge(ident_ok, 3)
            pool.affine_select(out=ident[:, :], in_=ident[:, :], compare_op=ALU.not_equal, fill=1.0, base=0,
                               pattern=[[-1, P]], channel_multiplier=1).then_inc(ident_ok, 1)
            pool.wait_ge(ident_ok, 4)

            def split(hi, lo, slot, loads, before):
                pool.wait_ge(raw_in[slot], loads)
                nc.gpsimd.tensor_tensor(hi, stage[:, slot], one[:, 0:1].unsqueeze(2).broadcast_to([P, 2, QT]),
                                        ALU.mult).then_inc(hi_done, 1)
                pool.wait_ge(hi_done, before + 1)
                nc.gpsimd.tensor_tensor(lo, stage[:, slot], hi, ALU.subtract).then_inc(split_done, 1)

            for half in range(2):
                pool.wait_ge(bn_done, (2 * HB + 1) * (half + 1))
                seqs = slice(half * HB, (half + 1) * HB)
                nc.gpsimd.tensor_tensor(rstd[:, seqs], rstd[:, seqs], mhalf[:, :].broadcast_to([P, HB]), ALU.pow) \
                    .then_inc(rstd_done, 1)
            for n in range(NW):
                w, c = (wk, wv)[n // 2], 2 * (n % 2)
                split(w[:, 0, c:c + 2, :], w[:, 1, c:c + 2, :], n % 2, 16 * (n // 2 + 1), n)
            with pool.Fori(0, B) as b:
                for k in range(LB):
                    g, c = k // 2, 2 * (k % 2)
                    if c == 0:
                        pool.wait_ge(proj_done, b * GB + GQ * (g + 1))
                    split(ctx_h[:, g % 2, c:c + 2, :], ctx_l[:, g % 2, c:c + 2, :], k % 2,
                          b * (16 * LB // 2) + 16 * (NW // 2 + k // 2 + 1), b * LB + (NW + k))

        @block.tensor
        def _(pe):
            pe.wait_ge(ident_ok, 4)
            for half in range(2):
                for i in range(HB):
                    n = half * HB + i
                    pe.wait_ge(xn_done, n + 1)
                    if n >= 2:
                        pe.wait_ge(xT_copied, n - 1)
                    for c in range(DC):
                        last = nc.tensor.transpose(ps_t[:, n % 2, c, :], x_all[:, n, c * P:(c + 1) * P], ident[:, :])
                    last.then_inc(xT_done, 1)
                pe.wait_ge(wq_in, 16)
                pe.wait_ge(xT_copied, (half + 1) * HB)
                for p in range(PAIRS):
                    if half:
                        pe.wait_ge(q_lo, p + 1)
                    for c in range(DC):
                        last = nc.tensor.matmul(ps_s[:, p, :], wq[:, c, p * P:(p + 1) * P], xnT[:, c, :],
                                                start=(c == 0), stop=(c == DC - 1))
                    last.then_inc(qp_done, 1)
            pe.wait_ge(q_lo, 2 * PAIRS)

            def three(out, w_hi, w_lo, m_hi, m_lo):
                for c in range(DC):
                    for k, (w, m) in enumerate(((w_hi, m_hi), (w_hi, m_lo), (w_lo, m_hi))):
                        mm = nc.tensor.matmul(out, w(c), m(c), start=(c + k == 0), stop=(c == DC - 1 and k == 2))
                return mm

            with pe.Fori(0, B) as b:
                def scores(h):
                    for j in range(4):
                        if h == 0:
                            pe.wait_ge(k_lo, b * (NQ * PAIRS) + ((NQ - 1) * PAIRS + j + 1))
                        else:
                            pe.wait_ge(exp_done, AHEAD + b * (2 * XH) + (2 * (h - 1) + j // 2 + 1))
                        keys = kT[:, h % 2, h // 2, j * 512:(j + 1) * 512]
                        nc.tensor.matmul(ps_s[:, j, :], qa[:, h, :], keys, start=True, stop=False)
                        mm = nc.tensor.matmul(ps_s[:, j, :], qb[:, h, :], keys, start=False, stop=True)
                        if j % 2:
                            mm.then_inc(s_done, 1)

                pe.wait_ge(exp_done, AHEAD + b * (2 * XH))
                for g in range(NQ):
                    pe.wait_ge(split_done, b * LB + (NW + 2 * (g + 1)))
                    h, l = ctx_h[:, g % 2], ctx_l[:, g % 2]
                    for p in range(PAIRS):
                        if g:
                            pe.wait_ge(k_lo, b * (NQ * PAIRS) + (PAIRS * (g - 1) + p + 1))
                        cols = slice(p * P, (p + 1) * P)
                        three(ps_s[:, p, :], lambda c: wk[:, 0, c, cols], lambda c: wk[:, 1, c, cols],
                              lambda c: h[:, c, :], lambda c: l[:, c, :]).then_inc(proj_done, 1)
                    for t in range(4):
                        if g or t >= 2:
                            pe.wait_ge(v_copied, b * MT + (4 * g + t - 1))
                        if g == NQ - 1 and t == 2:
                            pe.wait_ge(q_in, (b + 1) * (16 * 8))
                            scores(0)
                        rows = slice(t * P, (t + 1) * P)
                        mm = three(ps_v[:, t % 2, :], lambda c: h[:, c, rows], lambda c: l[:, c, rows],
                                   lambda c: wv[:, 0, c, :], lambda c: wv[:, 1, c, :])
                        mm.then_inc(proj_done, 1)

                def transposes(h):
                    e = h % 2
                    for j in range(4):
                        if j % 2 == 0:
                            pe.wait_ge(exp_done, AHEAD + b * (2 * XH) + (2 * h + j // 2 + 1))
                        n = 4 * h + j
                        if n < 2:
                            pe.wait_ge(v_copied, (b + 1) * MT)
                        elif n == 2:
                            pe.wait_ge(r_copied, b + AHEAD)
                        else:
                            h3, j3 = (n - 3) // 4, (n - 3) % 4
                            pe.wait_ge((pT_even, pT_odd)[h3 % 2], AHEAD + b * MT + (4 * (h3 // 2) + j3 + 1))
                        for i in range(4):
                            mm = nc.tensor.transpose(ps_t[:, n % 3, i, :],
                                                     probs[:, e, (4 * j + i) * P:(4 * j + i + 1) * P], ident[:, :])
                        mm.then_inc(t_done, 1)

                def values(p, part):
                    if p == 0 and part == 0:
                        pe.wait_ge(on_done, AHEAD + b)
                        pe.wait_ge(v_copied, (b + 1) * MT)
                    pe.wait_ge(pT_even, AHEAD + b * MT + (4 * p + 2 * (part + 1)))
                    pe.wait_ge(pT_odd, AHEAD + b * MT + (4 * p + 2 * (part + 1)))
                    for t in range(8 * part, 8 * part + 8):
                        for e in range(2):
                            h = 2 * p + e
                            mm = nc.tensor.matmul(ps_o[e * XD:(e + 1) * XD, p, :], vt[:, t, h * XD:(h + 1) * XD],
                                                  pT[:, e, t, :], start=(t == 0), stop=(t == MT - 1))
                    return mm

                pe.wait_ge(k_lo, (b + 1) * (NQ * PAIRS))
                for p in range(PAIRS):
                    if p:
                        scores(2 * p)
                    if p:
                        transposes(2 * p - 1)
                        values(p - 1, 0)
                    scores(2 * p + 1)
                    if p:
                        values(p - 1, 1)
                    transposes(2 * p)
                transposes(XH - 1)
                values(PAIRS - 1, 0)
                values(PAIRS - 1, 1).then_inc(pv_done, 1)
                pe.wait_ge(spread_done, b + 1)
                for p in range(PAIRS):
                    mm = nc.tensor.matmul(ps_r[:, p, :], spread[:, 2 * p:2 * p + 2, :].rearrange("p h d -> p (h d)"),
                                          ident[:, :], start=True, stop=True)
                mm.then_inc(r_done, 1)

        @block.scalar
        def _(act):
            act.dma_start(x_all[:, HB:B], x_ap[HB:B].rearrange("b t d -> t b d")).then_inc(x_in[1], 16)
            act.sem_inc(proj_done, 2 * GQ)
            for n in range(2 * PAIRS):
                act.wait_ge(qp_done, n + 1)
                nc.scalar.activation(q_halves[:, 0, n * HT:(n + 1) * HT], ps_s[:, n % PAIRS, :], ACT.Copy) \
                    .then_inc(q_hi, 1)
                if n % PAIRS == PAIRS - 1:
                    half = n // PAIRS
                    act.wait_ge(q_lo, n + 1)
                    for w in range(2):
                        act.dma_start(q_dram[w, :, :, half * HT:(half + 1) * HT].rearrange("h p t -> p h t"),
                                      q_halves[:, w, half * PAIRS * HT:(half + 1) * PAIRS * HT]
                                      .rearrange("p (h t) -> p h t", h=PAIRS).bitcast(F32)).then_inc(q_stored, 16)
            act.wait_ge(q_stored, 16 * 4)
            with act.Fori(0, B) as b:
                act.wait_ge(s_done, AHEAD + b * (2 * XH))
                for w, dst in enumerate((qa, qb)):
                    d = dst[:, :, :].bitcast(F32).rearrange("p (h e) t -> p h e t", e=2)
                    for e in range(2):
                        for to in range(2):
                            act.dma_start(d[to * XD:(to + 1) * XD, :, e, :],
                                          q_dram[w, :, e * XD:(e + 1) * XD, bass.ds(b * T, T)]
                                          .rearrange("h p t -> p h t")).then_inc(q_in, 16)
                def exps(h):
                    act.wait_ge(nmax_done, b * XH + (h + 1))
                    for j in range(2):
                        nc.scalar.activation(probs[:, h % 2, j * 1024:(j + 1) * 1024], ps_s[:, 2 * j:2 * j + 2, :],
                                             ACT.Exp, bias=nmax[:, h:h + 1], scale=X_SCALE,
                                             accum_out=rsum[:, h, j:j + 1]).then_inc(exp_done, 1)

                for g in range(NQ):
                    keys = slice(g * QT, (g + 1) * QT)
                    for p in range(PAIRS):
                        act.wait_ge(proj_done, b * GB + (GQ * (g + 2) + p + 1))
                        nc.scalar.activation(kT[0:XD, 0, p, keys], ps_s[0:XD, p, :], ACT.Copy)
                        nc.scalar.activation(kT[XD:P, 1, p, keys], ps_s[XD:P, p, :], ACT.Copy).then_inc(k_hi, 1)
                    for t in range(4):
                        if g == NQ - 1 and t == 3:
                            exps(0)
                        act.wait_ge(proj_done, b * GB + (GQ * (g + 2) + PAIRS + t + 1))
                        nc.scalar.activation(vt[:, 4 * g + t, :], ps_v[:, t % 2, :], ACT.Copy).then_inc(v_copied, 1)

                def copy_odd(p):
                    for j in range(4):
                        act.wait_ge(t_done, b * (4 * XH) + (4 * (2 * p + 1) + j + 1))
                        nc.scalar.activation(pT[:, 1, 4 * j:4 * j + 4, :], ps_t[:, (4 * (2 * p + 1) + j) % 3, :, :], ACT.Copy) \
                            .then_inc(pT_odd, 1)

                for p in range(PAIRS):
                    if p:
                        copy_odd(p - 1)
                        exps(2 * p)
                    exps(2 * p + 1)
                copy_odd(PAIRS - 1)
                act.wait_ge(on_done, AHEAD + b + 1)
                act.dma_start(o_dram[bass.ds(b, 1)].rearrange("o p h t -> (o p) h t"), on[:, :, :]) \
                    .then_inc(o_stored, 16)
            act.wait_ge(o_stored, AHEAD + 16 * B)

        @block.vector
        def _(dve):
            for half in range(2):
                before = (2 * HB + 1) * half
                seqs = range(half * HB, (half + 1) * HB)
                dve.wait_ge(x_in[half], 16)
                for n in seqs:
                    nc.vector.bn_stats(stats[:, n, :], x_all[:, n, :]).then_inc(bn_done, 1)
                for i, n in enumerate(seqs):
                    dve.wait_ge(bn_done, before + i + 1)
                    nc.vector.bn_aggr(mv[:, n, :], stats[:, n, :]).then_inc(bn_done, 1)
                dve.wait_ge(bn_done, before + 2 * HB)
                nc.vector.tensor_scalar(rstd[:, half * HB:(half + 1) * HB], mv[:, half * HB:(half + 1) * HB, 1], EPS,
                                        None, ALU.add).then_inc(bn_done, 1)
            for n in range(B):
                if n % HB == 0:
                    dve.wait_ge(rstd_done, n // HB + 1)
                nc.vector.tensor_scalar(x_all[:, n, :], x_all[:, n, :], mv[:, n, 0:1], rstd[:, n:n + 1],
                                        ALU.subtract, ALU.mult).then_inc(xn_done, 1)

            def q_low(n):
                dve.wait_ge(q_hi, n + 1)
                cols = slice(n * HT, (n + 1) * HT)
                nc.vector.tensor_tensor(q_halves[:, 1, cols], ps_s[:, n % PAIRS, :], q_halves[:, 0, cols],
                                        ALU.subtract).then_inc(q_lo, 1)

            for half in range(2):
                for i in range(HB):
                    n = half * HB + i
                    dve.wait_ge(xT_done, n + 1)
                    if half and i == 0:
                        dve.wait_ge(qp_done, PAIRS)
                    nc.vector.tensor_copy(xnT[:, :, i * T:(i + 1) * T], ps_t[:, n % 2, :, :]).then_inc(xT_copied, 1)
                for p in range(PAIRS):
                    q_low(half * PAIRS + p)

            with dve.Fori(0, B) as b:
                for g in range(NQ):
                    keys = slice(g * QT, (g + 1) * QT)
                    for p in range(PAIRS):
                        dve.wait_ge(k_hi, b * (NQ * PAIRS) + (PAIRS * g + p + 1))
                        nc.vector.tensor_tensor(kT[XD:P, 0, p, keys], ps_s[0:XD, p, :], kT[0:XD, 0, p, keys],
                                                ALU.subtract)
                        nc.vector.tensor_tensor(kT[0:XD, 1, p, keys], ps_s[XD:P, p, :], kT[XD:P, 1, p, keys],
                                                ALU.subtract).then_inc(k_lo, 1)

                def maxes(h):
                    for j in range(2):
                        dve.wait_ge(s_done, AHEAD + b * (2 * XH) + (2 * h + j + 1))
                        nc.vector.tensor_reduce(smax[:, h, j:j + 1], ps_s[:, 2 * j:2 * j + 2, :]
                                                .rearrange("p a n -> p (a n)"), AX_X, ALU.max).then_inc(max_done, 1)
                    dve.wait_ge(max_done, b * (2 * XH) + 2 * (h + 1))
                    nc.vector.tensor_scalar(nmax[:, h:h + 1], smax[:, h, 0:1], smax[:, h, 1:2], -X_SCALE,
                                            ALU.max, ALU.mult).then_inc(nmax_done, 1)

                def copy_even(p):
                    for j in range(4):
                        dve.wait_ge(t_done, b * (4 * XH) + (4 * (2 * p) + j + 1))
                        nc.vector.tensor_copy(pT[:, 0, 4 * j:4 * j + 4, :], ps_t[:, (4 * (2 * p) + j) % 3, :, :]).then_inc(pT_even, 1)

                for p in range(PAIRS):
                    maxes(2 * p)
                    maxes(2 * p + 1)
                    copy_even(p)
                dve.wait_ge(exp_done, AHEAD + (b + 1) * (2 * XH))
                nc.vector.tensor_tensor(rtot[:, :], rsum[:, :, 0], rsum[:, :, 1], ALU.add).then_inc(sum_done, 1)
                dve.wait_ge(sum_done, 2 * b + 1)
                nc.vector.reciprocal(rinv[:, :], rtot[:, :]).then_inc(sum_done, 1)
                dve.wait_ge(sum_done, 2 * b + 2)
                nc.vector.tensor_copy(spread[:, :, :], rinv[:, :].unsqueeze(2).broadcast_to([P, XH, XD])) \
                    .then_inc(spread_done, 1)
                dve.wait_ge(o_stored, AHEAD + b * 16)
                dve.wait_ge(r_done, b + 1)
                nc.vector.tensor_copy(on[:, :, :], ps_r).then_inc(r_copied, 1)
                dve.wait_ge(r_copied, b + (AHEAD + 1))
                nc.vector.tensor_tensor(on[:, :, :], ps_o[:, :, :], on[:, :, :], ALU.mult).then_inc(on_done, 1)


def self_attention(nc, x_ap, bo_ap, wxo_ap, wq_ap, wkd_ap, wvd_ap, wku_ap, wvu_ap, wo_ap, wg_ap, up_ap, down_ap,
                   o_dram, rows_dram, x2, xn3, logits, wu, wd, w_loaded):
    with ExitStack() as ctx:
        def sb(name, shape, dt=F32):
            return ctx.enter_context(nc.sbuf_tensor(name, shape, dt))

        def sem(name):
            return ctx.enter_context(nc.semaphore(name))

        DC2 = SH * SD // P
        wxo = sb("wxo", [P, PAIRS, D])
        wq = sb("wq2", [P, DC, SH * SD])
        wdown = sb("wdown", [P, DC, 4 * LAT])
        wup = sb("wup", [P, 4, SD])
        wo = sb("wo2", [P, DC2, D])
        wg = sb("wg", [P, DC, E])
        bo = sb("bo", [P, D])
        ident = sb("ident2", [P, P])
        mask = sb("mask", [P, P])
        mhalf = sb("mhalf2", [P, 1])
        hold = sb("hold", [P, 1])
        o_in = sb("o_in", [P, B, PAIRS, P])
        xnT = sb("xnT", [P, B, DC, T])
        qT = sb("qT", [P, SH, T])
        lat = sb("lat", [P, 1, T])
        kT = sb("kT2", [P, SKV, T])
        v = sb("v2", [P, SKV, SD])
        sm = sb("sm", [P, SKV, REP, T])
        pT = sb("pT2", [P, SKV, REP, T])
        yT = sb("yT", [P, SH, T])
        x3T = sb("x3T", [P, 2, DC, T])
        stats = sb("stats2", [P, 2, 6])
        mv = sb("mv2", [P, 2, 2])
        rstd = sb("rstd2", [P, 2, 1])
        mx = sb("mx2", [P, SKV, REP])
        sums = sb("sums2", [P, SKV, REP])
        inv = sb("inv2", [P, SKV, REP])

        banks = [ctx.enter_context(nc.psum_tensor(f"bank{i}", [P, 512], F32)) for i in range(8)]

        HOLDS = (("lat", "v"), ("qa", "kT"), ("qb",), ("sc0",), ("sc1",), ("pT0", "y0"), ("pT1", "y1"), ("wo",))
        OUT, XT, X3T, LG = (6, 7), (0, 1), (0, 1), (2, 3)
        filled = [sem(f"filled{i}") for i in range(8)]
        copied = [sem(f"copied{i}") for i in range(8)]

        def place(name, s):
            for par in range(2):
                if name == f"out{par}":
                    return OUT[par], s
                if name == f"xT{par}":
                    return XT[par], s
                if name == f"x3T{par}":
                    return X3T[par], s + (B // 2 + B * len(HOLDS[X3T[par]]))
                if name == f"lg{par}":
                    return LG[par], s + B * len(HOLDS[LG[par]])
            i = next(i for i, names in enumerate(HOLDS) if name in names)
            before = B // 2 if i in OUT + XT else 0
            return i, s * len(HOLDS[i]) + (before + HOLDS[i].index(name))

        def bank(name):
            return banks[place(name, 0)[0]][:, :]

        def await_filled(eng, name, s):
            i, n = place(name, s)
            eng.wait_ge(filled[i], n + 1)

        def await_copied(eng, name, s):
            i, n = place(name, s)
            eng.wait_ge(copied[i], n + (AHEAD + 1))

        def await_empty(eng, name, s):
            i, n = place(name, s)
            eng.wait_ge(copied[i], n + AHEAD)

        def fill(mm, name):
            mm.then_inc(filled[place(name, 0)[0]], 1)

        bo_in = sem("bo_in")
        wxo_in = sem("wxo_in")
        wq_in = sem("wq_in2")
        wkv_in = sem("wkv_in")
        wo_in = sem("wo_in")
        wup_zero = sem("wup_zero")
        consts = sem("consts")
        o_got = [sem("o_got0"), sem("o_got1"), sem("o_got2")]
        x_got = sem("x_got")
        xb_done = sem("xb_done")
        dve_step = sem("dve_step")
        var_done = sem("var_done")
        rstd_done = sem("rstd_done2")
        xn_done = sem("xn_done2")
        sub_done = sem("sub_done")
        exp_done = sem("exp_done2")
        p_done = sem("p_done")
        xn3_stored = sem("xn3_stored")

        block = ctx.enter_context(nc.Block())

        @block.sync
        def _(sp):
            sp.dma_start(wxo[:, :, :], wxo_ap.rearrange("(c p) n -> p c n", p=P)).then_inc(wxo_in, 16)
            sp.dma_start(bo[:, :], bo_ap.rearrange("(a n) -> a n", a=1).broadcast_to([P, D])).then_inc(bo_in, 16)
            for i, ap in enumerate((wkd_ap, wvd_ap)):
                sp.dma_start(wdown[:, :, 2 * LAT * i:2 * LAT * (i + 1)], ap.rearrange("(c p) n -> p c n", p=P)) \
                    .then_inc(wkv_in, 16)
            sp.wait_ge(wup_zero, 1)
            for i in range(4):
                sp.dma_start(wup[LAT * i:LAT * (i + 1), i, :], (wku_ap, wvu_ap)[i // 2]).then_inc(wkv_in, 16)
            sp.dma_start(wq[:, :, :], wq_ap.rearrange("(c p) n -> p c n", p=P)).then_inc(wq_in, 16)
            for w, ap in ((wo, wo_ap), (wg, wg_ap)):
                sp.dma_start(w[:, :, :], ap.rearrange("(c p) n -> p c n", p=P)).then_inc(wo_in, 16)
            for s in range(2):
                sp.dma_start(wu[:, s], up_ap[s].rearrange("(c p) n -> p c n", p=P)).then_inc(w_loaded[s], 16)
                sp.dma_start(wd[:, s], down_ap[s].rearrange("(c p) n -> p c n", p=P)).then_inc(w_loaded[s], 16)
            sp.wait_ge(xn_done, 2 * B)
            sp.dma_start(rows_dram[0:B].rearrange("s t d -> t s d"), xn3[:, :, :]).then_inc(xn3_stored, 16)
            sp.wait_ge(xn3_stored, 16)
            for s in range(2):
                sp.wait_ge(w_loaded[s], 32)

        @block.gpsimd
        def _(pool):
            for count in copied:
                pool.sem_inc(count, AHEAD)
            pool.memset(mhalf[:, :], -0.5).then_inc(consts, 1)
            pool.memset(ident[:, :], 0.0).then_inc(consts, 1)
            pool.memset(mask[:, :], 0.0).then_inc(consts, 1)
            pool.wait_ge(bo_in, 16)
            pool.wait_ge(x_got, 16)
            for s in range(B):
                nc.gpsimd.tensor_tensor(x2[:, s, :], x2[:, s, :], bo[:, :], ALU.add).then_inc(xb_done, 1)
                if s == 0:
                    pool.wait_ge(consts, 3)
                    pool.memset(wup[:, :, :], 0.0).then_inc(wup_zero, 1)
                    pool.affine_select(out=ident[:, :], in_=ident[:, :], compare_op=ALU.not_equal, fill=1.0, base=0,
                                       pattern=[[-1, P]], channel_multiplier=1).then_inc(consts, 1)
                    pool.affine_select(out=mask[:, :], in_=mask[:, :], compare_op=ALU.is_ge, fill=-3.0e38, base=0,
                                       pattern=[[-1, P]], channel_multiplier=1).then_inc(consts, 1)
                pool.wait_ge(var_done, s + 1)
                nc.gpsimd.tensor_tensor(rstd[:, s % 2, :], rstd[:, s % 2, :], mhalf[:, :], ALU.pow) \
                    .then_inc(rstd_done, 1)
            with pool.Fori(0, B) as s:
                pool.wait_ge(var_done, s + (B + 1))
                nc.gpsimd.tensor_tensor(rstd[:, 0, :], rstd[:, 0, :], mhalf[:, :], ALU.pow).then_inc(rstd_done, 1)

        @block.tensor
        def _(pe):
            def accumulate(out, pieces):
                for c, (w, m) in enumerate(pieces):
                    mm = nc.tensor.matmul(out, w, m, start=(c == 0), stop=(c == len(pieces) - 1))
                return mm

            def transpose_all(name, tiles):
                for c, tile in enumerate(tiles):
                    mm = nc.tensor.transpose(bank(name)[:, c * P:(c + 1) * P], tile, ident[:, :])
                fill(mm, name)

            def turn_norm(name, s, n, wait):
                await_empty(pe, name, n)
                pe.wait_ge(xn_done, wait)
                transpose_all(name, [xn3[:, s, c * P:(c + 1) * P] for c in range(DC)])

            def normed(s, c):
                return xnT[:, bass.ds(s, 1), c, :].rearrange("p o t -> p (o t)")

            def queries(name, s, n):
                await_empty(pe, name, s)
                for i in range(4):
                    h = 4 * n + i
                    mm = accumulate(bank(name)[:, i * T:(i + 1) * T],
                                    [(wq[:, c, h * SD:(h + 1) * SD], normed(s, c)) for c in range(DC)])
                fill(mm, name)

            def turn_probs(s):
                for g in range(SKV):
                    await_empty(pe, f"pT{g}", s)
                    pe.wait_ge(p_done, s * SKV + (g + 1))
                    transpose_all(f"pT{g}", [sm[:, g, r, :] for r in range(REP)])

            def values(s):
                await_copied(pe, "v", s)
                for g in range(SKV):
                    await_copied(pe, f"pT{g}", s)
                    fill(accumulate(bank(f"y{g}"), [(v[:, g, :], pT[:, g, :, :])]), f"y{g}")

            def project(s):
                await_empty(pe, "wo", s)
                for g in range(SKV):
                    await_copied(pe, f"y{g}", s)
                fill(accumulate(bank("wo"), [(yT[:, h, :], wo[:, h, :]) for h in range(SH)]), "wo")

            def step(s, before=None):
                queries("qa", s, 0)
                await_empty(pe, "lat", s)
                fill(accumulate(bank("lat")[:, 0:T], [(wdown[:, c, :], normed(s, c)) for c in range(DC)]), "lat")
                if before is not None:
                    turn_probs(before)
                queries("qb", s, 1)
                await_copied(pe, "lat", s)
                await_empty(pe, "kT", s)
                for g in range(SKV):
                    mm = accumulate(bank("kT")[:, g * T:(g + 1) * T], [(wup[:, g, :], lat[:, 0, :])])
                fill(mm, "kT")
                if before is not None:
                    values(before)
                fill(accumulate(bank("v")[:, 0:SKV * SD], [(lat[:, 0, :], wup[:, 2:4, :])]), "v")
                for name in ("qa", "qb", "kT"):
                    await_copied(pe, name, s)
                for g in range(SKV):
                    await_empty(pe, f"sc{g}", s)
                    for r in range(REP):
                        mm = accumulate(bank(f"sc{g}")[:, r * T:(r + 1) * T], [(qT[:, g * REP + r, :], kT[:, g, :])])
                    fill(mm, f"sc{g}")
                if before is not None:
                    project(before)

            def route(s):
                i, par = s // 2, s % 2
                await_empty(pe, f"lg{par}", i)
                await_copied(pe, f"x3T{par}", i)
                fill(accumulate(bank(f"lg{par}")[:, 0:E], [(x3T[:, par, c, :], wg[:, c, :]) for c in range(DC)]),
                     f"lg{par}")

            pe.wait_ge(wxo_in, 16)
            for s in range(B):
                name = f"out{s % 2}"
                pe.wait_ge(o_got[min(s, 2)], 16)
                await_empty(pe, name, s // 2)
                fill(accumulate(bank(name), [(o_in[:, s, p, :], wxo[:, p, :]) for p in range(PAIRS)]), name)
                if s == 1:
                    pe.wait_ge(consts, 5)
                if s >= 2:
                    turn_norm(f"xT{s % 2}", s - 2, s // 2 - 1, s - 1)
            pe.wait_ge(wq_in, 16)
            pe.wait_ge(wkv_in, 16 * 6)
            for s in (B - 2, B - 1):
                turn_norm(f"xT{s % 2}", s, s // 2, s + 1)
            for par in range(2):
                await_copied(pe, f"xT{par}", B // 2 - 1)
            step(0)
            pe.wait_ge(wo_in, 32)
            with pe.Fori(1, B) as s:
                step(s, before=s - 1)
            turn_probs(B - 1)
            values(B - 1)
            project(B - 1)
            for s in range(B):
                i, par = s // 2, s % 2
                turn_norm(f"x3T{par}", s, i, B + s + 1)
                if s:
                    route(s - 1)
            route(B - 1)

        @block.scalar
        def _(act):
            def take(name, s, dst):
                n = dst.shape[1] * dst.shape[2]
                await_filled(act, name, s)
                nc.scalar.activation(dst, bank(name)[:, 0:n].rearrange("p (a t) -> p a t", a=dst.shape[1]),
                                     ACT.Copy).then_inc(copied[place(name, 0)[0]], 1)

            def step(s, before=None):
                take("qa", s, qT[:, 0:4])
                take("lat", s, lat[:, :])
                if before is not None:
                    take("pT0", before, pT[:, 0])
                take("qb", s, qT[:, 4:8])
                take("kT", s, kT[:, :])
                if before is not None:
                    take("y0", before, yT[:, 0:REP])
                take("v", s, v[:, :])
                for g in range(SKV):
                    act.wait_ge(sub_done, s * SKV + (g + 1))
                    t = sm[:, g]
                    nc.scalar.activation(t, t, ACT.Exp).then_inc(exp_done, 1)

            for n, (a, b) in enumerate(((0, 1), (1, 2), (2, B))):
                act.dma_start(o_in[:, a:b], o_dram[a:b].rearrange("s p h t -> p s h t")).then_inc(o_got[n], 16)
                if n == 0:
                    act.dma_start(x2[:, :, :], x_ap.rearrange("s t d -> t s d")).then_inc(x_got, 16)
            for s in range(B):
                take(f"xT{s % 2}", s // 2, xnT[:, s])
            step(0)
            with act.Fori(1, B) as s:
                step(s, before=s - 1)
            take("pT0", B - 1, pT[:, 0])
            take("y0", B - 1, yT[:, 0:REP])
            for s in range(B):
                take(f"x3T{s % 2}", s // 2, x3T[:, s % 2])

        @block.vector
        def _(dve):
            def take(name, s, dst):
                n = dst.shape[1] * dst.shape[2]
                await_filled(dve, name, s)
                nc.vector.tensor_copy(dst, bank(name)[:, 0:n].rearrange("p (a t) -> p a t", a=dst.shape[1])) \
                    .then_inc(copied[place(name, 0)[0]], 1)

            def add(name, n, s, par, linked):
                row = x2[:, bass.ds(s, 1), :].rearrange("p o d -> p (o d)")
                await_filled(dve, name, n)
                nc.vector.tensor_tensor(row, bank(name), row, ALU.add).then_inc(copied[place(name, 0)[0]], 1)
                await_copied(dve, name, n)
                nc.vector.memset(hold[:, :], 0.0)
                nc.vector.bn_stats(stats[:, par, :], row).then_inc(dve_step, 1)
                dve.wait_ge(dve_step, linked + 1)
                nc.vector.memset(hold[:, :], 0.0)
                nc.vector.bn_aggr(mv[:, par, :], stats[:, par, :]).then_inc(dve_step, 1)
                dve.wait_ge(dve_step, linked + 2)
                nc.vector.tensor_scalar(rstd[:, par, :], mv[:, par, 1:2], EPS, None, ALU.add).then_inc(var_done, 1)

            def norm(s, par, n):
                row = x2[:, bass.ds(s, 1), :].rearrange("p o d -> p (o d)")
                dve.wait_ge(rstd_done, n + 1)
                nc.vector.tensor_scalar(xn3[:, bass.ds(s, 1), :].rearrange("p o d -> p (o d)"), row, mv[:, par, 0:1],
                                        rstd[:, par, :], ALU.subtract, ALU.mult).then_inc(xn_done, 1)

            LN = 2
            FRONT, BACK = 2, 4
            per_step = LN + FRONT + BACK

            def shift(s, linked):
                for g in range(SKV):
                    await_filled(dve, f"sc{g}", s)
                    t = sm[:, g]
                    nc.vector.scalar_tensor_tensor(
                        out=t, in0=bank(f"sc{g}").rearrange("p (r t) -> p r t", r=REP), scalar=S_SCALE,
                        in1=mask[:, :].unsqueeze(1).broadcast_to([P, REP, T]), op0=ALU.mult, op1=ALU.add) \
                        .then_inc(copied[place(f"sc{g}", 0)[0]], 1)
                    await_copied(dve, f"sc{g}", s)
                    nc.vector.tensor_reduce(mx[:, g, :], t, AX_X, ALU.max).then_inc(dve_step, 1)
                    dve.wait_ge(dve_step, linked + (g + 1))
                    nc.vector.tensor_tensor(t, t, mx[:, g, :].unsqueeze(2).broadcast_to([P, REP, T]),
                                            ALU.subtract).then_inc(sub_done, 1)

            def normalise(s, linked):
                for g in range(SKV):
                    dve.wait_ge(exp_done, s * SKV + (g + 1))
                    t = sm[:, g]
                    nc.vector.tensor_reduce(sums[:, g, :], t, AX_X, ALU.add).then_inc(dve_step, 1)
                    dve.wait_ge(dve_step, linked + (2 * g + 1))
                    nc.vector.reciprocal(inv[:, g, :], sums[:, g, :]).then_inc(dve_step, 1)
                    dve.wait_ge(dve_step, linked + (2 * g + 2))
                    nc.vector.tensor_tensor(t, t, inv[:, g, :].unsqueeze(2).broadcast_to([P, REP, T]),
                                            ALU.mult).then_inc(p_done, 1)

            for s in range(B):
                dve.wait_ge(xb_done, s + 1)
                add(f"out{s % 2}", s // 2, s, s % 2, LN * s)
                if s:
                    norm(s - 1, (s - 1) % 2, s - 1)
            norm(B - 1, (B - 1) % 2, B - 1)
            base = LN * B
            shift(0, base)
            normalise(0, base + FRONT)
            base += FRONT + BACK
            with dve.Fori(1, B) as s:
                linked = (s - 1) * per_step + base
                take("pT1", s - 1, pT[:, 1])
                take("y1", s - 1, yT[:, REP:SH])
                shift(s, linked)
                add("wo", s - 1, s - 1, 0, linked + FRONT)
                normalise(s, linked + (FRONT + LN))
                norm(s - 1, 0, s + (B - 1))
            base += (B - 1) * per_step
            take("pT1", B - 1, pT[:, 1])
            take("y1", B - 1, yT[:, REP:SH])
            add("wo", B - 1, B - 1, 0, base)
            norm(B - 1, 0, 2 * B - 1)
            for s in range(B):
                name = f"lg{s % 2}"
                await_filled(dve, name, s // 2)
                nc.vector.tensor_copy(logits[:, s, :], bank(name)[:, 0:E]).then_inc(copied[place(name, 0)[0]], 1)


def experts(nc, up_ap, down_ap, out_ap, rows_dram, x2, xn3, logits, wu, wd, w_loaded):
    with ExitStack() as ctx:
        def sb(name, shape, dt=F32):
            return ctx.enter_context(nc.sbuf_tensor(name, shape, dt))

        def sem(name):
            return ctx.enter_context(nc.semaphore(name))

        FC = F // P
        NT = B * T // P
        ident = sb("ident3", [P, P])
        before = sb("before", [P, P])
        ones = sb("ones3", [P, P])
        row = sb("row", [P, D])
        rowT = sb("rowT", [P, DC, P])
        gT = sb("gT", [P, FC, P])
        y = sb("y", [P, D])
        picked = sb("picked", [P, 2, NT, D])
        hold = sb("hold3", [P, 1])
        iota = sb("iota", [P, E])
        thr = sb("thr", [P, NT - 1])
        probs = sb("probs3", [P, NT, E])
        lmax = sb("lmax", [P, NT])
        den = sb("den", [P, NT])
        rden = sb("rden3", [P, NT])
        top = sb("top", [P, NT, 8])
        index = sb("index", [P, NT, 8], U32)
        index_f = sb("index_f", [P, NT, 2])
        weight = sb("weight", [P, NT, 2])
        hit = sb("hit", [P, 2, NT, E])
        both = sb("both", [P, NT, E])
        rank = sb("rank", [P, NT, E])
        earlier = sb("earlier", [P, NT + 1, E])
        full = sb("full", [P, E, NT - 1])
        n_tiles = sb("n_tiles", [P, E])
        first = sb("first", [P, E + 1])
        first_i = sb("first_i", [P, E + 1], U32)
        slot = sb("slot", [P, 2, NT])
        slot_i = sb("slot_i", [P, 2, NT], U32)

        up_ps = ctx.enter_context(nc.psum_tensor("up_ps", [P, 2, 4, P], F32))
        down_ps = ctx.enter_context(nc.psum_tensor("down_ps", [P, D], F32))
        rowT_ps = ctx.enter_context(nc.psum_tensor("rowT_ps", [P, DC, P], F32))
        rank_ps = ctx.enter_context(nc.psum_tensor("rank_ps", [P, NT, E], F32, ))
        total_ps = ctx.enter_context(nc.psum_tensor("total_ps", [P, 512], F32))

        consts = sem("consts3")
        route = sem("route")
        e_done = sem("e_done")
        hits_done = sem("hits_done")
        counted = sem("counted")
        slots_done = sem("slots_done")
        firsts_done = sem("firsts_done")
        rows_sent = sem("rows_sent")
        row_in = sem("row_in")
        rowT_done = sem("rowT_done")
        rowT_copied = sem("rowT_copied")
        up_done = sem("up_done")
        gelu_done = sem("gelu_done")
        down_done = sem("down_done")
        y_copied = sem("y_copied")
        y_stored = sem("y_stored")
        got = [sem(f"got{t}") for t in range(NT)]
        mixed = sem("mixed")
        out_stored = sem("out_stored")

        block = ctx.enter_context(nc.Block())

        def bounds(eng, e):
            lo = eng.value_load(first_i[0:1, bass.ds(e, 1)], min_val=NT, max_val=MAX_TILES)
            hi = eng.value_load(first_i[0:1, bass.ds(e + 1, 1)], min_val=NT + 1, max_val=MAX_TILES)
            return lo, hi

        @block.sync
        def _(sp):
            def load_weights(s, par, done):
                sp.wait_ge(down_done, done)
                sp.dma_start(wu[:, par], up_ap[bass.ds(s, 1)].rearrange("o (c p) n -> p (o c) n", p=P)) \
                    .then_inc(w_loaded[par], 16)
                sp.dma_start(wd[:, par], down_ap[bass.ds(s, 1)].rearrange("o (c p) n -> p (o c) n", p=P)) \
                    .then_inc(w_loaded[par], 16)

            def store_tiles(e):
                with sp.Fori(*bounds(sp, e)) as t:
                    sp.wait_ge(y_copied, t + (AHEAD + 1))
                    sp.dma_start(rows_dram[bass.ds(t, 1)].rearrange("o p d -> (o p) d"), y[:, :]).then_inc(y_stored, 16)

            sp.wait_ge(firsts_done, 1)
            with sp.Fori(0, E // 2 - 1) as j:
                for k in range(2):
                    done = sp.value_load(first_i[0:1, bass.ds(j * 2 + k, 1)], min_val=NT, max_val=MAX_TILES)
                    load_weights(j * 2 + (k + 2), k, done)
                    store_tiles(j * 2 + k)
            done = sp.value_load(first_i[0:1, E - 2:E - 1], min_val=NT, max_val=MAX_TILES)
            load_weights(E, 0, done)
            for e in (E - 2, E - 1):
                store_tiles(e)
            for t in range(NT):
                sp.wait_ge(mixed, 2 * (t + 1))
                sp.dma_start(out_ap[t], x2[:, t, :]).then_inc(out_stored, 16)
            sp.wait_ge(out_stored, 16 * NT)

        @block.gpsimd
        def _(pool):
            pool.sem_inc(y_stored, 16 * NT)
            pool.memset(ident[:, :], 0.0).then_inc(consts, 1)
            pool.memset(before[:, :], 0.0).then_inc(consts, 1)
            pool.memset(ones[:, :], 1.0).then_inc(consts, 1)
            pool.memset(hold[:, :], 0.0).then_inc(consts, 1)
            pool.iota(iota[:, :], pattern=[[1, E]], base=0, channel_multiplier=0,
                      allow_small_or_imprecise_dtypes=True).then_inc(consts, 1)
            pool.iota(thr[:, :], pattern=[[P, NT - 1]], base=P, channel_multiplier=0,
                      allow_small_or_imprecise_dtypes=True).then_inc(consts, 1)
            pool.wait_ge(consts, 6)
            pool.affine_select(out=ident[:, :], in_=ident[:, :], compare_op=ALU.not_equal, fill=1.0, base=0,
                               pattern=[[-1, P]], channel_multiplier=1).then_inc(consts, 1)
            pool.affine_select(out=before[:, :], in_=before[:, :], compare_op=ALU.is_ge, fill=1.0, base=0,
                               pattern=[[-1, P]], channel_multiplier=1).then_inc(consts, 1)
            pool.wait_ge(slots_done, 1)
            for t in range(NT):
                for k in range(2):
                    pool.indirect_dma_start(
                        out=rows_dram.rearrange("n p d -> (n p) d"),
                        out_offset=bass.IndirectOffsetOnAxis(ap=slot_i[:, k, t:t + 1], axis=0),
                        in_=xn3[:, t, :], in_offset=None).then_inc(rows_sent, 16)
            pool.wait_ge(firsts_done, 1)
            pool.wait_ge(rows_sent, 16 * 2 * NT)
            end = pool.value_load(first_i[0:1, E:E + 1], min_val=NT, max_val=MAX_TILES)
            pool.wait_ge(y_stored, end * 16)
            nc.gpsimd.tensor_tensor(hold[:, :], hold[:, :], hold[:, :], ALU.add)
            for t in range(NT):
                for k in range(2):
                    pool.indirect_dma_start(
                        out=picked[:, k, t, :], out_offset=None,
                        in_=rows_dram.rearrange("n p d -> (n p) d"),
                        in_offset=bass.IndirectOffsetOnAxis(ap=slot_i[:, k, t:t + 1], axis=0)).then_inc(got[t], 16)

        @block.tensor
        def _(pe):
            def turn(n):
                pe.wait_ge(row_in, n * 16 + 16)
                pe.wait_ge(rowT_copied, n + AHEAD)
                for c in range(DC):
                    mm = nc.tensor.transpose(rowT_ps[:, c, :], row[:, c * P:(c + 1) * P], ident[:, :])
                mm.then_inc(rowT_done, 1)

            def tile(t, par):
                pe.wait_ge(rowT_copied, t + (AHEAD + 1))
                for n in range(2):
                    pe.wait_ge(gelu_done, t * 2 + (n + 1 - 2 + 2 * AHEAD))
                    for i in range(4):
                        f = 4 * n + i
                        for c in range(DC):
                            mm = nc.tensor.matmul(up_ps[:, n, i, :], wu[:, par, c, f * P:(f + 1) * P], rowT[:, c, :],
                                                  start=(c == 0), stop=(c == DC - 1))
                    mm.then_inc(up_done, 1)
                turn(t + 1)
                pe.wait_ge(y_copied, t + AHEAD)
                for f in range(FC):
                    if f % 4 == 0:
                        pe.wait_ge(gelu_done, t * 2 + (f // 4 + 1 + AHEAD))
                    mm = nc.tensor.matmul(down_ps[:, :], gT[:, f, :], wd[:, par, f, :],
                                          start=(f == 0), stop=(f == FC - 1))
                mm.then_inc(down_done, 1)

            pe.wait_ge(consts, 8)
            turn(0)
            tile(0, 0)
            pe.wait_ge(hits_done, 1)
            nc.tensor.matmul(rank_ps[:, :, :], before[:, :], both[:, :, :], start=True, stop=True)
            nc.tensor.matmul(total_ps[:, 0:NT * E], ones[:, :], both[:, :, :], start=True, stop=True) \
                .then_inc(counted, 1)
            with pe.Fori(1, NT) as t:
                tile(t, 0)
            pe.wait_ge(firsts_done, 1)
            with pe.Fori(0, E // 2) as j:
                for k in range(2):
                    with pe.Fori(*bounds(pe, j * 2 + k)) as t:
                        pe.wait_ge(w_loaded[1 - k], j * 32 + (32 + 32 * k))
                        tile(t, 1 - k)

        @block.scalar
        def _(act):
            def load_row(n):
                act.dma_start(row[:, :], rows_dram[bass.ds(n, 1)].rearrange("o p d -> (o p) d")).then_inc(row_in, 16)

            def tile(t, before_load=None):
                act.wait_ge(rowT_done, t + 1)
                if before_load:
                    before_load()
                load_row(t + 1)
                for n in range(2):
                    act.wait_ge(up_done, t * 2 + (n + 1))
                    nc.scalar.activation(gT[:, 4 * n:4 * n + 4, :], up_ps[:, n], ACT.Gelu).then_inc(gelu_done, 1)

            act.sem_inc(gelu_done, AHEAD)
            act.dma_start(row[:, :], rows_dram[0]).then_inc(row_in, 16)
            act.wait_ge(route, 2)
            nc.scalar.activation(probs[:, :, :], probs[:, :, :], ACT.Exp).then_inc(e_done, 1)
            with act.Fori(0, NT - 1) as t:
                tile(t)
            tile(NT - 1, lambda: act.wait_ge(rows_sent, 16 * 2 * NT))
            act.wait_ge(firsts_done, 1)
            with act.Fori(0, E) as e:
                with act.Fori(*bounds(act, e)) as t:
                    tile(t)
            act.wait_ge(row_in, 16)

        @block.vector
        def _(dve):
            steps = [0]

            def link(ins):
                steps[0] += 1
                ins.then_inc(route, 1)
                dve.wait_ge(route, steps[0])

            def copy_rowT(n):
                dve.wait_ge(rowT_done, n + 1)
                nc.vector.tensor_copy(rowT[:, :, :], rowT_ps[:, :, :]).then_inc(rowT_copied, 1)

            def add_shared(t):
                dve.wait_ge(down_done, t + 1)
                x2t = x2[:, bass.ds(t, 1), :].rearrange("p o d -> p (o d)")
                nc.vector.tensor_tensor(x2t, down_ps[:, :], x2t, ALU.add).then_inc(y_copied, 1)

            def spread(ap):
                return ap.unsqueeze(2).broadcast_to([P, NT, E])

            dve.sem_inc(rowT_copied, AHEAD)
            dve.sem_inc(y_copied, AHEAD)
            copy_rowT(0)
            link(nc.vector.tensor_reduce(lmax[:, :], logits[:, :, :], AX_X, ALU.max))
            link(nc.vector.tensor_tensor(probs[:, :, :], logits[:, :, :], spread(lmax[:, :]), ALU.subtract))
            dve.wait_ge(e_done, 1)
            link(nc.vector.tensor_reduce(den[:, :], probs[:, :, :], AX_X, ALU.add))
            link(nc.vector.reciprocal(rden[:, :], den[:, :]))
            link(nc.vector.tensor_tensor(probs[:, :, :], probs[:, :, :], spread(rden[:, :]), ALU.mult))
            for t in range(NT):
                last = nc.vector.max(top[:, t, :], probs[:, t, :])
            link(last)
            for t in range(NT):
                last = nc.vector.max_index(index[:, t, :], top[:, t, :], probs[:, t, :])
            link(last)
            link(nc.vector.tensor_copy(index_f[:, :, :], index[:, :, 0:2]))
            dve.wait_ge(consts, 8)
            for k in range(2):
                link(nc.vector.tensor_tensor(hit[:, k], iota[:, :].unsqueeze(1).broadcast_to([P, NT, E]),
                                             index_f[:, :, k:k + 1].broadcast_to([P, NT, E]), ALU.is_equal))
            nc.vector.tensor_tensor(both[:, :, :], hit[:, 0], hit[:, 1], ALU.add).then_inc(hits_done, 1)
            link(nc.vector.tensor_tensor(den[:, :], top[:, :, 0], top[:, :, 1], ALU.add))
            link(nc.vector.reciprocal(rden[:, :], den[:, :]))
            link(nc.vector.tensor_tensor(weight[:, :, :], top[:, :, 0:2], rden[:, :].unsqueeze(2)
                                         .broadcast_to([P, NT, 2]), ALU.mult))
            link(nc.vector.memset(earlier[:, 0, :], 0.0))
            link(nc.vector.memset(first[:, 0:1], float(NT)))
            copy_rowT(1)
            add_shared(0)
            dve.wait_ge(counted, 1)
            for t in range(NT):
                link(nc.vector.tensor_tensor(earlier[:, t + 1, :], total_ps[:, t * E:(t + 1) * E], earlier[:, t, :],
                                             ALU.add))
            link(nc.vector.tensor_tensor(full[:, :, :], earlier[:, NT, :].unsqueeze(2).broadcast_to([P, E, NT - 1]),
                                         thr[:, :].unsqueeze(1).broadcast_to([P, E, NT - 1]), ALU.is_gt))
            link(nc.vector.tensor_reduce(n_tiles[:, :], full[:, :, :], AX_X, ALU.add))
            for e in range(E):
                link(nc.vector.tensor_scalar(first[:, e + 1:e + 2], n_tiles[:, e:e + 1], first[:, e:e + 1], 1.0,
                                             ALU.add, ALU.add))
            nc.vector.tensor_copy(first_i[:, :], first[:, :]).then_inc(firsts_done, 1)
            link(nc.vector.tensor_tensor(rank[:, :, :], rank_ps[:, :, :], earlier[:, 0:NT, :], ALU.add))
            link(nc.vector.scalar_tensor_tensor(out=rank[:, :, :], in0=first[:, 0:E].unsqueeze(1)
                                                .broadcast_to([P, NT, E]), scalar=float(P), in1=rank[:, :, :],
                                                op0=ALU.mult, op1=ALU.add))
            for k in range(2):
                link(nc.vector.tensor_tensor(hit[:, k], hit[:, k], rank[:, :, :], ALU.mult))
                link(nc.vector.tensor_reduce(slot[:, k, :], hit[:, k], AX_X, ALU.add))
            nc.vector.tensor_copy(slot_i[:, :, :], slot[:, :, :]).then_inc(slots_done, 1)
            with dve.Fori(1, NT) as t:
                copy_rowT(t + 1)
                add_shared(t)
            dve.wait_ge(firsts_done, 1)
            with dve.Fori(0, E) as e:
                with dve.Fori(*bounds(dve, e)) as t:
                    copy_rowT(t + 1)
                    dve.wait_ge(down_done, t + 1)
                    dve.wait_ge(y_stored, t * 16)
                    nc.vector.tensor_copy(y[:, :], down_ps[:, :]).then_inc(y_copied, 1)
            for t in range(NT):
                dve.wait_ge(got[t], 32)
                for k in range(2):
                    nc.vector.scalar_tensor_tensor(out=x2[:, t, :], in0=picked[:, k, t, :], scalar=weight[:, t, k:k + 1],
                                                   in1=x2[:, t, :], op0=ALU.mult, op1=ALU.add).then_inc(mixed, 1)
                    if k == 0:
                        dve.wait_ge(mixed, 2 * t + 1)


def perceiver_block(nc, x, ctx_t, xq, xk, xv, xo, xbo, sq, skd, svd, sku, svu, so, gate, up, down, out):
    q_dram = nc.dram_tensor("q_scratch", (2, PAIRS, P, B * T), F32, kind="Internal").ap()
    o_dram = nc.dram_tensor("o_scratch", (B, P, PAIRS, T), F32, kind="Internal").ap()
    rows_dram = nc.dram_tensor("rows_scratch", (MAX_TILES + 1, P, D), F32, kind="Internal").ap()
    cross_attention(nc, x, ctx_t, xq, xk, xv, q_dram, o_dram, rows_dram)
    with ExitStack() as ctx:
        x2 = ctx.enter_context(nc.sbuf_tensor("x2", [P, B, D], F32))
        xn3 = ctx.enter_context(nc.sbuf_tensor("xn3", [P, B, D], F32))
        logits = ctx.enter_context(nc.sbuf_tensor("logits", [P, B, E], F32))
        wu = ctx.enter_context(nc.sbuf_tensor("wu", [P, 2, DC, F], F32))
        wd = ctx.enter_context(nc.sbuf_tensor("wd", [P, 2, F // P, D], F32))
        w_loaded = [ctx.enter_context(nc.semaphore(f"w_loaded{i}")) for i in range(2)]
        self_attention(nc, x, xbo, xo, sq, skd, svd, sku, svu, so, gate, up, down, o_dram, rows_dram,
                       x2, xn3, logits, wu, wd, w_loaded)
        experts(nc, up, down, out, rows_dram, x2, xn3, logits, wu, wd, w_loaded)


def kernel(**inputs):
    import numpy as _np
    import concourse.bacc as _bacc
    from concourse import mybir as _mybir
    from concourse.bass_utils import run_bass_kernel_spmd as _run

    a = {k: _np.asarray(v) for k, v in inputs.items()}
    ctx_t = a["ctx_1024"].reshape(B, NQ, QT, DC, P).transpose(0, 1, 4, 3, 2)
    laid = [
        ("x", a["x"]), ("ctx", ctx_t), ("xq", a["L0_xattn_Wq"]), ("xk", a["L0_xattn_Wk"]),
        ("xv", a["L0_xattn_Wv"]), ("xo", a["L0_xattn_Wo"]), ("xbo", a["L0_xattn_bo"]),
        ("sq", a["L0_attn_wq"]), ("skd", a["L0_attn_wk_down"]), ("svd", a["L0_attn_wv_down"]),
        ("sku", a["L0_attn_wk_up"]), ("svu", a["L0_attn_wv_up"]), ("so", a["L0_attn_wo"]),
        ("gate", a["L0_ffn_Wg"]),
        ("up", _np.concatenate([a["L0_ffn_W1"][None], a["L0_ffn_Wu"]])),
        ("down", _np.concatenate([a["L0_ffn_W2"][None], a["L0_ffn_Wd"]])),
    ]
    nc = _bacc.Bacc("TRN2", target_bir_lowering=False, num_devices=1, dynamic_dma_scratch_size=4096)
    arrays, args = {}, []
    for name, v in laid:
        v = _np.ascontiguousarray(v)
        arrays[f"in_{name}_dram"] = v
        args.append(nc.dram_tensor(f"in_{name}_dram", v.shape, _mybir.dt.from_np(v.dtype), kind="ExternalInput").ap())
    args.append(nc.dram_tensor("out_0_dram", (B, T, D), _mybir.dt.float32, kind="ExternalOutput").ap())
    perceiver_block(nc, *args)
    r = _run(nc, [arrays], core_ids=[0])
    return r.results[0]["out_0_dram"]
```
